# Optimizing a Trainium2 kernel written in Bass

```python
import numpy as np
import jax
import jax.numpy as jnp

def _softmax(x, axis=-1):
    return jax.nn.softmax(x, axis=axis)
def _gelu(x):
    return jax.nn.gelu(x, approximate=True)
def _silu(x):
    return jax.nn.silu(x)
def _sigmoid(x):
    return jax.nn.sigmoid(x)
def _layernorm(x, axis=-1, eps=1e-5):
    m = jnp.mean(x, axis=axis, keepdims=True)
    v = jnp.var(x, axis=axis, keepdims=True)
    return (x - m) / jnp.sqrt(v + eps)
def _scatter_add(tgt, idx, src, axis=0):
    return tgt.at[idx].add(src)
def _segment_sum(src, seg, n):
    return jax.ops.segment_sum(src, seg, n)

kernel_name = 'mk_conv_preact_d4_conv_nchw16_536d5a'

def setup_inputs(seed: int = 0):
    np.random.seed(seed)
    _w = jnp.asarray
    def _rec_inputs():
        import jax
        import jax.numpy as jnp
        _gk = jax.random.key(seed)
        x = -9.26e-05 + 0.9999 * jax.random.normal(jax.random.fold_in(_gk, 1), (16, 16, 384, 384), jnp.float32)
        return x
    x = _rec_inputs()
    def _L0_conv_setup():
        import jax, jax.numpy as jnp
        import numpy as np
        B, CIN, COUT, K, H, W_SP = (16, 16, 16, 3, 384, 384)
        key = jax.random.key(seed)
        k1, k2 = jax.random.split(key)
        x = jax.random.normal(k1, (B, CIN, H, W_SP), dtype=jnp.float32)
        W = jax.random.normal(k2, (COUT, CIN, K, K), dtype=jnp.float32) * 0.05
        return {'x': x, 'W': W}
    _L0_conv_all = _L0_conv_setup()
    _L0_conv_in = {k: v for k, v in _L0_conv_all.items() if k in ('W', )}
    del _L0_conv_all

    def _L1_conv_setup():
        import jax, jax.numpy as jnp
        import numpy as np
        B, CIN, COUT, K, H, W_SP = (16, 16, 16, 3, 384, 384)
        key = jax.random.key(seed)
        k1, k2 = jax.random.split(key)
        x = jax.random.normal(k1, (B, CIN, H, W_SP), dtype=jnp.float32)
        W = jax.random.normal(k2, (COUT, CIN, K, K), dtype=jnp.float32) * 0.05
        return {'x': x, 'W': W}
    _L1_conv_all = _L1_conv_setup()
    _L1_conv_in = {k: v for k, v in _L1_conv_all.items() if k in ('W', )}
    del _L1_conv_all

    def _L2_conv_setup():
        import jax, jax.numpy as jnp
        import numpy as np
        B, CIN, COUT, K, H, W_SP = (16, 16, 16, 3, 384, 384)
        key = jax.random.key(seed)
        k1, k2 = jax.random.split(key)
        x = jax.random.normal(k1, (B, CIN, H, W_SP), dtype=jnp.float32)
        W = jax.random.normal(k2, (COUT, CIN, K, K), dtype=jnp.float32) * 0.05
        return {'x': x, 'W': W}
    _L2_conv_all = _L2_conv_setup()
    _L2_conv_in = {k: v for k, v in _L2_conv_all.items() if k in ('W', )}
    del _L2_conv_all

    def _L3_conv_setup():
        import jax, jax.numpy as jnp
        import numpy as np
        B, CIN, COUT, K, H, W_SP = (16, 16, 16, 3, 384, 384)
        key = jax.random.key(seed)
        k1, k2 = jax.random.split(key)
        x = jax.random.normal(k1, (B, CIN, H, W_SP), dtype=jnp.float32)
        W = jax.random.normal(k2, (COUT, CIN, K, K), dtype=jnp.float32) * 0.05
        return {'x': x, 'W': W}
    _L3_conv_all = _L3_conv_setup()
    _L3_conv_in = {k: v for k, v in _L3_conv_all.items() if k in ('W', )}
    del _L3_conv_all

    return {
        "x": x,
        "L0_conv_W": _L0_conv_in["W"],
        "L1_conv_W": _L1_conv_in["W"],
        "L2_conv_W": _L2_conv_in["W"],
        "L3_conv_W": _L3_conv_in["W"],
    }

def reference(x, L0_conv_W, L1_conv_W, L2_conv_W, L3_conv_W):
    import jax
    import jax.numpy as jnp
    def _L0_conv_ref(x, W):
        import jax, jax.numpy as jnp
        import numpy as np
        B, CIN, COUT, K, H, W_SP = (16, 16, 16, 3, 384, 384)
        b, cin, h, w = x.shape
        cout, _, kh, kw = W.shape
        mask = (x >= 0).astype(x.dtype)
        att = mask.reshape(b, cin, kh, h // kh, kw, w // kw).mean(axis=(3, 5))
        att = att.reshape(b, cin, kh * kw)
        att = kh * kw * jax.nn.softmax(att, axis=2) - 1.0
        att = 1.0 + jax.nn.sigmoid(att).reshape(b, cin, kh, kw)
        wmod = W[None, :, :, :, :] * att[:, None, :, :, :]

        def conv_one(xi, wi):
            return jax.lax.conv_general_dilated(xi[None], wi, window_strides=(1, 1), padding=[(1, 1), (1, 1)], dimension_numbers=('NCHW', 'OIHW', 'NCHW'))[0]
        y = jax.vmap(conv_one)(x, wmod)
        return y

    def _L1_conv_ref(x, W):
        import jax, jax.numpy as jnp
        import numpy as np
        B, CIN, COUT, K, H, W_SP = (16, 16, 16, 3, 384, 384)
        b, cin, h, w = x.shape
        cout, _, kh, kw = W.shape
        mask = (x >= 0).astype(x.dtype)
        att = mask.reshape(b, cin, kh, h // kh, kw, w // kw).mean(axis=(3, 5))
        att = att.reshape(b, cin, kh * kw)
        att = kh * kw * jax.nn.softmax(att, axis=2) - 1.0
        att = 1.0 + jax.nn.sigmoid(att).reshape(b, cin, kh, kw)
        wmod = W[None, :, :, :, :] * att[:, None, :, :, :]

        def conv_one(xi, wi):
            return jax.lax.conv_general_dilated(xi[None], wi, window_strides=(1, 1), padding=[(1, 1), (1, 1)], dimension_numbers=('NCHW', 'OIHW', 'NCHW'))[0]
        y = jax.vmap(conv_one)(x, wmod)
        return y

    def _L2_conv_ref(x, W):
        import jax, jax.numpy as jnp
        import numpy as np
        B, CIN, COUT, K, H, W_SP = (16, 16, 16, 3, 384, 384)
        b, cin, h, w = x.shape
        cout, _, kh, kw = W.shape
        mask = (x >= 0).astype(x.dtype)
        att = mask.reshape(b, cin, kh, h // kh, kw, w // kw).mean(axis=(3, 5))
        att = att.reshape(b, cin, kh * kw)
        att = kh * kw * jax.nn.softmax(att, axis=2) - 1.0
        att = 1.0 + jax.nn.sigmoid(att).reshape(b, cin, kh, kw)
        wmod = W[None, :, :, :, :] * att[:, None, :, :, :]

        def conv_one(xi, wi):
            return jax.lax.conv_general_dilated(xi[None], wi, window_strides=(1, 1), padding=[(1, 1), (1, 1)], dimension_numbers=('NCHW', 'OIHW', 'NCHW'))[0]
        y = jax.vmap(conv_one)(x, wmod)
        return y

    def _L3_conv_ref(x, W):
        import jax, jax.numpy as jnp
        import numpy as np
        B, CIN, COUT, K, H, W_SP = (16, 16, 16, 3, 384, 384)
        b, cin, h, w = x.shape
        cout, _, kh, kw = W.shape
        mask = (x >= 0).astype(x.dtype)
        att = mask.reshape(b, cin, kh, h // kh, kw, w // kw).mean(axis=(3, 5))
        att = att.reshape(b, cin, kh * kw)
        att = kh * kw * jax.nn.softmax(att, axis=2) - 1.0
        att = 1.0 + jax.nn.sigmoid(att).reshape(b, cin, kh, kw)
        wmod = W[None, :, :, :, :] * att[:, None, :, :, :]

        def conv_one(xi, wi):
            return jax.lax.conv_general_dilated(xi[None], wi, window_strides=(1, 1), padding=[(1, 1), (1, 1)], dimension_numbers=('NCHW', 'OIHW', 'NCHW'))[0]
        y = jax.vmap(conv_one)(x, wmod)
        return y

    def _gn(v, G=8, eps=1e-5):
        B_, C_, H_, W_ = v.shape
        g = v.reshape(B_, G, C_ // G, H_, W_)
        m = jnp.mean(g, axis=(2, 3, 4), keepdims=True)
        s = jnp.var(g, axis=(2, 3, 4), keepdims=True)
        return ((g - m) / jnp.sqrt(s + eps)).reshape(v.shape)

    def _ln_c(v, eps=1e-6):
        m = jnp.mean(v, axis=1, keepdims=True)
        s = jnp.var(v, axis=1, keepdims=True)
        return (v - m) / jnp.sqrt(s + eps)

    def _ln_t(v, eps=1e-5):
        m = jnp.mean(v, axis=-1, keepdims=True)
        s = jnp.var(v, axis=-1, keepdims=True)
        return (v - m) / jnp.sqrt(s + eps)

    def _to_tokens(v):
        B_, C_, H_, W_ = v.shape
        return v.reshape(B_, C_, H_ * W_).transpose(0, 2, 1)
    def _from_tokens(t, like):
        B_, C_, H_, W_ = like.shape
        return t.transpose(0, 2, 1).reshape(B_, C_, H_, W_)

    x = x + _L0_conv_ref(_gn(x), L0_conv_W)
    x = x + _L1_conv_ref(_gn(x), L1_conv_W)
    x = x + _L2_conv_ref(_gn(x), L2_conv_W)
    x = x + _L3_conv_ref(_gn(x), L3_conv_W)
    return x


_drawn_inputs = setup_inputs


def setup_inputs(seed=0):
    import zlib

    import numpy as np

    out = dict(_drawn_inputs(seed))
    spreads = {}
    factors = {}
    for name, (base, spread) in spreads.items():
        noise = np.random.default_rng([zlib.crc32(name.encode()), seed]).standard_normal(out[name].shape)
        drawn = base * np.exp(spread * noise) if base else spread * noise
        out[name] = jnp.asarray(drawn.astype(out[name].dtype))
    for name, factor in factors.items():
        out[name] = (out[name] * factor).astype(out[name].dtype)
    return out
```

```python
from contextlib import ExitStack

import concourse.bass as bass
from concourse import mybir

F32 = mybir.dt.float32
F16 = mybir.dt.float16
BF16 = mybir.dt.bfloat16
U8 = mybir.dt.uint8
ALU = mybir.AluOpType
ACT = mybir.ActivationFunctionType
AX = mybir.AxisListType

P = 128
B, C, H, W = 16, 16, 384, 384
L = 4
KK = 3
BR = P // C
NB = H // BR
TY = 4
NC = NB // TY
CH = TY * W
RING = 4
WP = W + 2
HS = BR * C * KK
GROUP = 2
GN = GROUP * H * W
AN = (H // KK) * (W // KK)
NR = KK * KK
EPS = 1e-5
WSCALE = 64.0
SMALL = 384

ROWS = []
for t in range(TY):
    inner = [(1, 2), (3, 4), (5, 6)]
    inner.insert(t, (0, 7))
    ROWS.append([r for pair in inner for r in pair])

NMASK = KK * TY * BR
CONSTS = 2 * P + NMASK + 2

MEAN_INCS = 2
PREP_INCS = 10
SCALE_INCS = 2
SPREAD_INCS = 5
WEIGHT_INCS = 2 * TY + 2
MODULATIONS = TY + 1
HALO_DMAS = 16
CHUNK_DMAS = 16


class Schedule:

    def __init__(self, mean_after, stats_after, counts, variances, splits):
        self.mean_after = mean_after
        self.stats_after = stats_after
        self.counts = counts
        self.variances = variances
        self.splits = splits


RESIDENT = Schedule(
    0, 8,
    {0: [0], 1: [1], 2: [2], 3: [3], 4: [4], 5: [5], 6: [6, 7], 7: [8]},
    {s: [2 * s - 2, 2 * s - 1] for s in range(1, 7)},
    {s: [s + RING] for s in range(NC)},
)
ARRIVING = Schedule(
    2, 9,
    {2: [0], 3: [1], 4: [2], 5: [3], 6: [4, 5], 7: [6, 7], 8: [8]},
    {3: [0, 1], 4: [2, 3], 5: [4, 5], 6: [6, 7], 7: [8, 9], 8: [10, 11]},
    {**{s: [s + RING] for s in range(NC - RING)}, 8: [], 9: [12, 13], 10: [14], 11: [15]},
)
SUM_LAG = 3


def build(nc, x_in, dense_in, border_in, const_in, out):
    with ExitStack() as ctx:
        def sb(name, shape, dt):
            return ctx.enter_context(nc.sbuf_tensor(name, shape, dt))

        def sem(name):
            return ctx.enter_context(nc.semaphore(name))

        img = [sb(f"image{p}", [P, NC * CH], F32) for p in range(2)]
        split = sb("split", [P, 2, RING * TY, WP], F16)
        halo = sb("halo", [96, RING * TY, WP], F16)
        normed = sb("normed", [P, CH], F32)
        wdense = [sb(f"wdense{p}", [P, 2, TY, HS], F16) for p in range(2)]
        wborder = [sb(f"wborder{p}", [96, KK * 2 * C], F16) for p in range(2)]
        dense = sb("dense", [P, TY, HS], F32)
        border = sb("border", [96, KK * 2 * C], F32)
        const = sb("const", [P, CONSTS], F32)
        zeros = sb("zeros", [C, 2 * WP], F16)
        over = sb("over", [P, TY * TY * (W // KK)], U8)
        dump = [sb(f"dump{i}", [P, CH], BF16) for i in range(3)]
        sums = [sb(f"sums{p}", [P, NC], F32) for p in range(2)]
        squares = sb("squares", [P, NC], F32)
        counts = sb("counts", [P, NR], F32)
        mean = sb("mean", [P, 1], F32)
        negmean = sb("negmean", [P, 1], F32)
        stats = sb("stats", [P, NC + NR], F32)
        var = sb("var", [P, 1], F32)
        vareps = sb("vareps", [P, 1], F32)
        scale = [sb(f"scale{p}", [P, 1], F32) for p in range(2)]
        shift = [sb(f"shift{p}", [P, 1], F32) for p in range(2)]
        top = sb("top", [P, 1], F32)
        att = [sb(f"att{i}", [P, NR], F32) for i in range(6)]
        esum = sb("esum", [P, 1], F32)
        erec = sb("erec", [P, 1], F32)
        spread = [sb(f"spread{i}", [P, TY, KK, BR], F32) for i in range(3)]
        ps = ctx.enter_context(nc.psum_tensor("ps", [P, 2, TY, 512], F32))

        group_m = const[:, 0:P]
        channel_m = const[:, P:2 * P]
        mask = const[:, 2 * P:2 * P + NMASK].rearrange("p (k t s) -> p k t s", k=KK, t=TY)
        neghalf = const[:, 2 * P + NMASK:2 * P + NMASK + 1]
        one = const[:, 2 * P + NMASK + 1:2 * P + NMASK + 2]

        const_loaded = sem("const_loaded")
        zeroed = sem("zeroed")
        loaded = [sem(f"loaded{i}") for i in range(4)]
        stored = [sem(f"stored{i}") for i in range(4)]
        fresh_summed = sem("fresh_summed")
        conv_done = sem("conv_done")
        banks_free = sem("banks_free")
        normed_done = sem("normed_done")
        high_done = sem("high_done")
        low_done = sem("low_done")
        halo_done = [sem(f"halo_done{i}") for i in range(RING)]
        mean_psum = sem("mean_psum")
        mean_ready = sem("mean_ready")
        counted = sem("counted")
        squared = sem("squared")
        stats_psum = sem("stats_psum")
        prep = sem("prep")
        scale_ready = sem("scale_ready")
        exps = sem("exps")
        spreaded = sem("spreaded")
        dense_loaded = sem("dense_loaded")
        modulated = sem("modulated")
        weights_ready = sem("weights_ready")

        def chunk(p, c):
            return img[p][:, c * CH:(c + 1) * CH]

        def max_zero(value):
            return max(value, 0) if isinstance(value, int) else value

        def rows4(ap):
            return ap.rearrange("p (b w) -> p b w", w=W)

        def ring_rows(part, slot):
            return split[:, part, slot * TY:(slot + 1) * TY, 1:1 + W]

        block = ctx.enter_context(nc.Block())

        @block.sync
        def _(sp):
            def transfer(p, c, image, store):
                for t in range(TY):
                    for q in reversed(range(BR // 2)):
                        a, b = ROWS[t][2 * q], ROWS[t][2 * q + 1]
                        row = (c * TY + t) * BR
                        tensor = out if store else x_in
                        dram = tensor[bass.ds(image, 1), :, row + a:row + b + 1:b - a, :].rearrange("i c s w -> (i c) s w")
                        sram = img[p][32 * q:32 * q + 32, c * CH + t * W:c * CH + (t + 1) * W]
                        if store:
                            sp.dma_start(dram, sram).then_inc(stored[c % 4], 16)
                        else:
                            sp.dma_start(sram, dram).then_inc(loaded[c % 4], 16)

            def store(p, c, pair, number):
                sp.wait_ge(banks_free, number + 3)
                transfer(p, c, 2 * pair + p, True)

            def load(p, c, pair):
                sp.wait_ge(stored[c % 4], 16 * CHUNK_DMAS * (3 * (2 * pair - 2 + p) + c // 4 + 1))
                transfer(p, c, 2 * pair + p, False)

            def send(c, t, side):
                slot = c % RING
                at = slot * TY + t
                to = (at + 1) % (RING * TY) if side == 0 else (at - 1) % (RING * TY)
                first = 32 * t + (1 if side == 0 else 0)
                both = split[first:first + 2 * C - 1:2, :, at, :]
                high = split[first:first + 2 * C - 1:2, 0, at, :]
                if c == 0 and t == 0 and side == 1:
                    side, to = 0, 0
                    both, high = zeros[:, :].rearrange("c (k w) -> c k w", k=2), zeros[:, 0:WP]
                if c == NC - 1 and t == TY - 1 and side == 0:
                    side, to = 1, at
                    both, high = zeros[:, :].rearrange("c (k w) -> c k w", k=2), zeros[:, 0:WP]
                sp.dma_start(halo[32 * side:32 * side + 32, to, :], both).then_inc(halo_done[slot], 16)
                sp.dma_start(halo[64 + side:64 + side + 2 * C - 1:2, to, :], high).then_inc(halo_done[slot], 16)

            def halo_sends(c, number):
                sp.wait_ge(high_done, number + 1)
                sp.wait_ge(low_done, number + 1)
                for t in range(TY):
                    for side in range(2):
                        if (t, side) != (TY - 1, 0):
                            send(c, t, side)

            def load_weights(layer, k):
                sp.wait_ge(weights_ready, WEIGHT_INCS * (k + 1))
                sp.dma_start(dense[:, :, :], dense_in[bass.ds(layer, 1), :, :].rearrange("l p (t n) -> (l p) t n", t=TY)).then_inc(dense_loaded, 16)
                sp.dma_start(border[:, :], border_in[bass.ds(layer, 1), :, :].rearrange("l p n -> (l p) n")).then_inc(dense_loaded, 16)

            def phase(sch, p, k, layer_after, jobs, last=False):
                for i in range(NC):
                    if i == 2:
                        load_weights(layer_after, k)
                    for q in sch.splits[i]:
                        halo_sends(q % NC, 12 * k + q)
                        if q == i + RING:
                            for job, jp, c, which in jobs.get(i, []):
                                if job == "store":
                                    store(jp, c, which, 12 * k + c)
                                else:
                                    load(jp, c, which)
                        if not (last and q == NC + RING - 1):
                            sp.wait_ge(conv_done, 12 * k + q - RING + 2)
                            send(q % NC, TY - 1, 0)
                    if i + RING not in sch.splits[i]:
                        for job, jp, c, which in jobs.get(i, []):
                            if job == "store":
                                store(jp, c, which, 12 * k + c)
                            else:
                                load(jp, c, which)

            sp.dma_start(const[:, :], const_in).then_inc(const_loaded, 16)
            sp.dma_start(dense[:, :, :], dense_in[0].rearrange("p (t n) -> p t n", t=TY)).then_inc(dense_loaded, 16)
            sp.dma_start(border[:, :], border_in[0]).then_inc(dense_loaded, 16)
            first = [(p, c) for p in range(2) for c in range(NC)][:-1]
            for n, (p, c) in enumerate(first[:16]):
                if n >= 4:
                    sp.wait_ge(fresh_summed, n - 3)
                transfer(p, c, p, False)
            sp.wait_ge(zeroed, 3)
            for q in range(RING):
                halo_sends(q, q)
                if q == RING - 1:
                    sp.wait_ge(conv_done, 1)
                send(q, TY - 1, 0)
            for n, (p, c) in enumerate(first):
                if n >= 16:
                    sp.wait_ge(fresh_summed, n - 3)
                    transfer(p, c, p, False)

            def head(pair):
                phase(ARRIVING, 0, 8 * pair, 0, {0: [("load", 1, NC - 1, pair)]})
                phase(RESIDENT, 1, 8 * pair + 1, 1, {})

            def middle(pair):
                with sp.Fori(1, L - 1) as layer:
                    phase(RESIDENT, 0, 8 * pair + 2 * layer, layer, {})
                    phase(RESIDENT, 1, 8 * pair + 2 * layer + 1, layer + 1, {})

            def tail(pair, more):
                even = {i: [("store", 0, i, pair)] + ([("load", 0, i - 1, pair + 1)] if more and i else []) for i in range(NC)}
                odd = {i: [("store", 1, i, pair)] + ([("load", 1, i - 1, pair + 1)] if more and i else []) for i in range(NC)}
                if more:
                    odd[0].append(("load", 0, NC - 1, pair + 1))
                phase(RESIDENT, 0, 8 * pair + 6, L - 1, even)
                phase(ARRIVING, 1, 8 * pair + 7, 0, odd, last=not more)

            with sp.Fori(0, B // 2 - 1) as pair:
                head(pair)
                middle(pair)
                tail(pair, True)
            head(B // 2 - 1)
            middle(B // 2 - 1)
            tail(B // 2 - 1, False)
            for i in range(4):
                sp.wait_ge(stored[i], 16 * CHUNK_DMAS * (NC // 4) * B)

        @block.scalar
        def _(act):
            def fresh(p, c, image):
                act.wait_ge(loaded[c % 4], 16 * CHUNK_DMAS * (3 * image + c // 4 + 1))
                act.wait_ge(fresh_summed, NC * image + c)
                nc.scalar.activation(dump[2][:, :], chunk(p, c), ACT.Identity,
                                     accum_out=sums[p][:, c:c + 1]).then_inc(fresh_summed, 1)

            def square(p, c, n):
                act.wait_ge(mean_ready, MEAN_INCS * (n + 1))
                act.wait_ge(squared, max_zero(NC * n + c - 1))
                nc.scalar.activation(dump[c % 2][:, :], chunk(p, c), ACT.Square, bias=negmean[:, :],
                                     accum_out=squares[:, c:c + 1]).then_inc(squared, 1)

            def normalise(p, c, number, free=None):
                if free is not None:
                    act.wait_ge(conv_done, free)
                act.wait_ge(low_done, number)
                nc.scalar.activation(normed[:, :], chunk(p, c), ACT.Identity, bias=shift[p][:, :],
                                     scale=scale[p][:, :]).then_inc(normed_done, 1)
                nc.scalar.activation(ring_rows(0, c % RING), rows4(chunk(p, c)), ACT.Identity, bias=shift[p][:, :],
                                     scale=scale[p][:, :]).then_inc(high_done, 1)

            def exp_shares(n):
                act.wait_ge(prep, PREP_INCS * n + 5)
                nc.scalar.activation(att[1][:, :], att[0][:, :], ACT.Exp, accum_out=esum[:, :]).then_inc(exps, 1)

            def exp_sigmoid(n):
                act.wait_ge(prep, PREP_INCS * n + 7)
                nc.scalar.activation(att[3][:, :], att[2][:, :], ACT.Exp, bias=one, scale=-float(NR)).then_inc(exps, 1)

            def phase(sch, p, k, sums_due):
                n = k + 1
                for i in range(NC):
                    if i == sch.stats_after:
                        exp_shares(n)
                        act.wait_ge(scale_ready, SCALE_INCS * (n + 1))
                    for q in sch.splits[i]:
                        normalise(p if q < NC else 1 - p, q % NC, 12 * k + q, 12 * k + q - RING + 1)
                    if i == sch.stats_after:
                        exp_sigmoid(n)
                    for fp, c, image in sums_due.get(i, []):
                        fresh(fp, c, image)
                    for c in sch.variances.get(i, []):
                        square(1 - p, c, n)

            act.wait_ge(const_loaded, 16)
            for c in range(NC):
                fresh(0, c, 0)
            for c in range(NC):
                square(0, c, 0)
            exp_shares(0)
            act.wait_ge(scale_ready, SCALE_INCS)
            act.wait_ge(zeroed, 3)
            for q in range(RING):
                normalise(0, q, q)
            exp_sigmoid(0)
            for c in range(NC - SUM_LAG):
                fresh(1, c, 1)

            def head(pair):
                phase(ARRIVING, 0, 8 * pair, {0: [(1, NC - 3, 2 * pair + 1)], 1: [(1, NC - 2, 2 * pair + 1), (1, NC - 1, 2 * pair + 1)]})
                phase(RESIDENT, 1, 8 * pair + 1, {})

            def middle(pair):
                with act.Fori(1, L - 1) as layer:
                    phase(RESIDENT, 0, 8 * pair + 2 * layer, {})
                    phase(RESIDENT, 1, 8 * pair + 2 * layer + 1, {})

            def tail(pair, more):
                even, odd = {}, {}
                if more:
                    even = {i: [(0, i - SUM_LAG, 2 * pair + 2)] for i in range(SUM_LAG, NC)}
                    odd = {i: [(1, i - SUM_LAG, 2 * pair + 3)] for i in range(SUM_LAG, NC)}
                    odd[0] = [(0, NC - 3, 2 * pair + 2)]
                    odd[1] = [(0, NC - 2, 2 * pair + 2), (0, NC - 1, 2 * pair + 2)]
                phase(RESIDENT, 0, 8 * pair + 6, even)
                if not more:
                    act.sem_inc(fresh_summed, NC)
                phase(ARRIVING, 1, 8 * pair + 7, odd)

            with act.Fori(0, B // 2 - 1) as pair:
                head(pair)
                middle(pair)
                tail(pair, True)
            head(B // 2 - 1)
            middle(B // 2 - 1)
            tail(B // 2 - 1, False)

        @block.vector
        def _(dve):
            def evacuate(p, c, number):
                dve.wait_ge(conv_done, number + 1)
                nc.vector.scalar_tensor_tensor(
                    out=rows4(chunk(p, c)), in0=ps[:, c % 2, :, 0:W], scalar=1.0 / WSCALE, in1=rows4(chunk(p, c)),
                    op0=ALU.mult, op1=ALU.add, accum_out=sums[p][:, c:c + 1]).then_inc(banks_free, 1)

            def low(c, number):
                dve.wait_ge(normed_done, number + 1)
                dve.wait_ge(high_done, number + 1)
                nc.vector.tensor_tensor(ring_rows(1, c % RING), rows4(normed[:, :]), ring_rows(0, c % RING),
                                        ALU.subtract).then_inc(low_done, 1)

            def take_mean(n, half):
                dve.wait_ge(mean_psum, n + 1)
                nc.vector.tensor_reduce(mean[:, :], ps[:, half, TY - 1, SMALL:SMALL + NC], AX.X, ALU.add).then_inc(mean_ready, 1)
                dve.wait_ge(mean_ready, MEAN_INCS * n + 1)
                nc.vector.tensor_scalar(negmean[:, :], mean[:, :], -1.0, None, ALU.mult).then_inc(mean_ready, 1)

            def count(p, r, n):
                v, h = divmod(r, KK)
                nb, w = NB // KK, W // KK
                dve.wait_ge(counted, NR * n + r)
                region = img[p][:, v * nb * W:(v + 1) * nb * W].rearrange("p (b w) -> p b w", w=W)[:, :, h * w:(h + 1) * w]
                nc.vector.tensor_scalar(over[:, :].rearrange("p (b w) -> p b w", w=w), region, mean[:, :], None,
                                        ALU.is_ge, ALU.add, accum_out=counts[:, r:r + 1]).then_inc(counted, 1)

            def take_stats(n, half):
                dve.wait_ge(stats_psum, n + 1)
                nc.vector.tensor_copy(stats[:, :], ps[:, half, TY - 1, SMALL:SMALL + NC + NR]).then_inc(prep, 1)
                dve.wait_ge(prep, PREP_INCS * n + 1)
                nc.vector.tensor_reduce(var[:, :], stats[:, 0:NC], AX.X, ALU.add).then_inc(prep, 1)
                dve.wait_ge(prep, PREP_INCS * n + 2)
                nc.vector.tensor_scalar(vareps[:, :], var[:, :], EPS, None, ALU.add).then_inc(prep, 1)
                nc.vector.tensor_reduce(top[:, :], stats[:, NC:NC + NR], AX.X, ALU.max).then_inc(prep, 1)
                dve.wait_ge(prep, PREP_INCS * n + 4)
                nc.vector.tensor_scalar(att[0][:, :], stats[:, NC:NC + NR], top[:, :], None, ALU.subtract).then_inc(prep, 1)

            def attention(n):
                dve.wait_ge(exps, 2 * n + 1)
                nc.vector.reciprocal(erec[:, :], esum[:, :]).then_inc(prep, 1)
                dve.wait_ge(prep, PREP_INCS * n + 6)
                nc.vector.tensor_scalar(att[2][:, :], att[1][:, :], erec[:, :], None, ALU.mult).then_inc(prep, 1)
                dve.wait_ge(exps, 2 * n + 2)
                nc.vector.tensor_scalar(att[4][:, :], att[3][:, :], 1.0, None, ALU.add).then_inc(prep, 1)
                dve.wait_ge(prep, PREP_INCS * n + 8)
                nc.vector.reciprocal(att[1][:, :], att[4][:, :]).then_inc(prep, 1)
                dve.wait_ge(prep, PREP_INCS * n + 9)
                nc.vector.tensor_scalar(att[5][:, :], att[1][:, :], WSCALE, WSCALE, ALU.mult, ALU.add).then_inc(prep, 1)

            def phase(sch, p, k):
                n = k + 1
                for i in range(NC):
                    evacuate(p, i, 12 * k + i)
                    if i == sch.mean_after:
                        take_mean(n, (i + 1) % 2)
                        dve.wait_ge(mean_ready, MEAN_INCS * (n + 1))
                    if i == sch.stats_after:
                        take_stats(n, (i + 1) % 2)
                    for q in sch.splits[i]:
                        low(q % NC, 12 * k + q)
                    if i == sch.stats_after:
                        attention(n)
                    for r in sch.counts.get(i, []):
                        count(1 - p, r, n)

            nc.vector.memset(split[:, :, :, :], 0.0).then_inc(zeroed, 1)
            nc.vector.memset(halo[:, :, :], 0.0).then_inc(zeroed, 1)
            nc.vector.memset(zeros[:, :], 0.0).then_inc(zeroed, 1)
            dve.sem_inc(banks_free, 2)
            take_mean(0, 0)
            dve.wait_ge(mean_ready, MEAN_INCS)
            for r in range(NR):
                count(0, r, 0)
            take_stats(0, 0)
            for q in range(RING):
                low(q, q)
            attention(0)

            with dve.Fori(0, B // 2) as pair:
                phase(ARRIVING, 0, 8 * pair)
                phase(RESIDENT, 1, 8 * pair + 1)
                with dve.Fori(1, L - 1) as layer:
                    phase(RESIDENT, 0, 8 * pair + 2 * layer)
                    phase(RESIDENT, 1, 8 * pair + 2 * layer + 1)
                phase(RESIDENT, 0, 8 * pair + 6)
                phase(ARRIVING, 1, 8 * pair + 7)

        @block.gpsimd
        def _(pool):
            def spread_attention(n):
                shape = [P, TY, KK, BR]
                value = att[5][:, :].rearrange("p (k x) -> p k x", k=KK)

                def by_ky(ky):
                    return (mask[:, ky, :, :].unsqueeze(2).to_broadcast(shape),
                            value[:, ky, :].unsqueeze(1).unsqueeze(3).to_broadcast(shape))

                base = SPREAD_INCS * n
                pool.wait_ge(prep, PREP_INCS * (n + 1))
                for ky in range(KK):
                    nc.gpsimd.tensor_tensor(spread[ky][:, :, :, :], *by_ky(ky), ALU.mult).then_inc(spreaded, 1)
                pool.wait_ge(spreaded, base + 3)
                nc.gpsimd.tensor_tensor(spread[0][:, :, :, :], spread[0][:, :, :, :], spread[1][:, :, :, :], ALU.add).then_inc(spreaded, 1)
                pool.wait_ge(spreaded, base + 4)
                nc.gpsimd.tensor_tensor(spread[0][:, :, :, :], spread[0][:, :, :, :], spread[2][:, :, :, :], ALU.add).then_inc(spreaded, 1)
                pool.wait_ge(spreaded, base + 5)

            def prepare(p, n):
                pool.wait_ge(prep, PREP_INCS * n + 3)
                nc.gpsimd.tensor_tensor(scale[p][:, :], vareps[:, :], neghalf, ALU.pow).then_inc(scale_ready, 1)
                pool.wait_ge(scale_ready, SCALE_INCS * n + 1)
                nc.gpsimd.tensor_tensor(shift[p][:, :], negmean[:, :], scale[p][:, :], ALU.mult).then_inc(scale_ready, 1)
                spread_attention(n)
                pool.wait_ge(dense_loaded, 32 * (n + 1))
                mods, ws = MODULATIONS * n, WEIGHT_INCS * n
                for t in range(TY):
                    factor = spread[0][:, t, :, :].rearrange("p x (q s) -> p (x q) s", s=2).unsqueeze(2)
                    factor = factor.to_broadcast([P, KK * BR // 2, C, 2])
                    d4 = dense[:, t, :].rearrange("p (a o s) -> p a o s", o=C, s=2)
                    h4 = wdense[p][:, 0, t, :].rearrange("p (a o s) -> p a o s", o=C, s=2)
                    nc.gpsimd.tensor_tensor(h4, d4, factor, ALU.mult).then_inc(weights_ready, 1)
                    nc.gpsimd.tensor_tensor(d4, d4, factor, ALU.mult).then_inc(modulated, 1)
                b4 = border[:, :].rearrange("p (x o s) -> p x o s", x=KK, s=2)
                bh4 = wborder[p][:, :].rearrange("p (x o s) -> p x o s", x=KK, s=2)
                value = att[5][0:96, :].rearrange("p (k x) -> p x k", k=KK)[:, :, 0:KK:2].unsqueeze(2).to_broadcast([96, KK, C, 2])
                nc.gpsimd.tensor_tensor(bh4, b4, value, ALU.mult).then_inc(weights_ready, 1)
                nc.gpsimd.tensor_tensor(b4, b4, value, ALU.mult).then_inc(modulated, 1)
                pool.wait_ge(weights_ready, ws + TY + 1)
                pool.wait_ge(modulated, mods + MODULATIONS)
                for t in range(TY):
                    nc.gpsimd.tensor_tensor(wdense[p][:, 1, t, :], dense[:, t, :], wdense[p][:, 0, t, :], ALU.subtract).then_inc(weights_ready, 1)
                pool.wait_ge(weights_ready, ws + 2 * TY + 1)
                nc.gpsimd.tensor_tensor(wborder[p][64:96, :], border[64:96, :], wborder[p][64:96, :], ALU.subtract).then_inc(weights_ready, 1)
                pool.wait_ge(weights_ready, ws + WEIGHT_INCS)

            pool.wait_ge(const_loaded, 16)
            prepare(0, 0)
            with pool.Fori(0, B // 2 * L) as m:
                prepare(1, 2 * m + 1)
                prepare(0, 2 * m + 2)

        @block.tensor
        def _(pe):
            def sum_means(p, n, half):
                nc.tensor.matmul(ps[:, half, TY - 1, SMALL:SMALL + NC], group_m, sums[p][:, :],
                                 start=True, stop=True).then_inc(mean_psum, 1)

            def sum_stats(n, half):
                pe.wait_ge(squared, NC * (n + 1))
                pe.wait_ge(counted, NR * (n + 1))
                nc.tensor.matmul(ps[:, half, TY - 1, SMALL:SMALL + NC], group_m, squares[:, :], start=True, stop=True)
                nc.tensor.matmul(ps[:, half, TY - 1, SMALL + NC:SMALL + NC + NR], channel_m, counts[:, :],
                                 start=True, stop=True).then_inc(stats_psum, 1)

            def convolve(p, c, number, guard=None):
                slot, half = c % RING, c % 2
                if c == 0:
                    pe.wait_ge(halo_done[0], 16 * HALO_DMAS * (number // RING + 1))
                if c < NC - 1:
                    pe.wait_ge(halo_done[(slot + 1) % RING], 16 * HALO_DMAS * ((number + 1) // RING + 1))
                pe.wait_ge(banks_free, number + 1)
                for t in range(TY):
                    if t == TY - 1 and guard is not None:
                        pe.wait_ge(*guard)
                    at = slot * TY + t
                    for kx in range(KK):
                        for w, v in ((1, 0), (0, 1), (0, 0)):
                            weights = wdense[p][:, w, t, kx * P:(kx + 1) * P]
                            nc.tensor.matmul(ps[:, half, t, 0:W], weights, split[:, v, at, kx:kx + W],
                                             start=(kx == 0 and w == 1), stop=False, skip_group_check=True)
                for kx in range(KK):
                    for t in range(TY):
                        last = nc.tensor.matmul(ps[32 * t:32 * t + 32, half, t, 0:W], wborder[p][:, kx * 2 * C:(kx + 1) * 2 * C],
                                                halo[:, slot * TY + t, kx:kx + W], start=False, stop=(kx == KK - 1), skip_group_check=True)
                last.then_inc(conv_done, 1)

            def phase(sch, p, k, wait_sums):
                n, g = k + 1, 12 * k
                pe.wait_ge(weights_ready, WEIGHT_INCS * (k + 1))
                for c in range(NC):
                    guard = None
                    if c == sch.mean_after + 1:
                        guard = (mean_ready, MEAN_INCS * n + 1)
                    if c == sch.stats_after + 1:
                        guard = (prep, PREP_INCS * n + 1)
                    convolve(p, c, g + c, guard)
                    if c == sch.mean_after:
                        pe.wait_ge(*wait_sums)
                        pe.wait_ge(banks_free, g + c + 2)
                        sum_means(1 - p, n, (c + 1) % 2)
                    if c == sch.stats_after:
                        pe.wait_ge(banks_free, g + c + 2)
                        sum_stats(n, (c + 1) % 2)

            def resident(p, k):
                phase(RESIDENT, p, k, (banks_free, 12 * k + 2))

            pe.wait_ge(const_loaded, 16)
            pe.wait_ge(fresh_summed, NC)
            sum_means(0, 0, 0)
            pe.wait_ge(mean_ready, 1)
            sum_stats(0, 0)
            pe.wait_ge(prep, 1)
            with pe.Fori(0, B // 2) as pair:
                phase(ARRIVING, 0, 8 * pair, (fresh_summed, NC * (2 * pair + 2)))
                resident(1, 8 * pair + 1)
                with pe.Fori(1, L - 1) as layer:
                    resident(0, 8 * pair + 2 * layer)
                    resident(1, 8 * pair + 2 * layer + 1)
                resident(0, 8 * pair + 6)
                phase(ARRIVING, 1, 8 * pair + 7, (fresh_summed, NC * (2 * pair + 3)))


def _layouts(weights):
    import numpy as np
    dense = np.zeros((L, BR // 2, C, 2, TY, KK, BR // 2, C, 2), np.float32)
    border = np.zeros((L, 96, KK, C, 2), np.float32)
    for layer, w in enumerate(weights):
        for t in range(TY):
            for si, ri in enumerate(ROWS[t]):
                for so, ro in enumerate(ROWS[t]):
                    ky = ri - ro + 1
                    if 0 <= ky < KK:
                        dense[layer, si // 2, :, si % 2, t, :, so // 2, :, so % 2] = w[:, :, ky, :].transpose(1, 2, 0)
        for side in range(2):
            taps = w[:, :, 2 * side, :].transpose(1, 2, 0)
            for part in range(2):
                border[layer, 32 * side + part:32 * side + 32:2, :, :, side] = taps
            border[layer, 64 + side:96:2, :, :, side] = taps
    return dense.reshape(L, P, TY * HS), border.reshape(L, 96, KK * 2 * C)


def _constants():
    import numpy as np
    part = np.arange(P)
    const = np.zeros((P, CONSTS), np.float32)
    channel = part % 32 // 2
    const[:, 0:P] = (channel[:, None] // GROUP == channel[None, :] // GROUP) / GN
    const[:, P:2 * P] = (channel[:, None] == channel[None, :]) / AN
    mask = np.zeros((P, KK, TY, BR), np.float32)
    for t in range(TY):
        for si, ri in enumerate(ROWS[t]):
            for so, ro in enumerate(ROWS[t]):
                if 0 <= ri - ro + 1 < KK:
                    mask[32 * (si // 2) + si % 2:32 * (si // 2) + 32:2, ri - ro + 1, t, so] = 1
    const[:, 2 * P:2 * P + NMASK] = mask.reshape(P, NMASK)
    const[:, 2 * P + NMASK] = -0.5
    const[:, 2 * P + NMASK + 1] = 1
    return const


def kernel(x, L0_conv_W, L1_conv_W, L2_conv_W, L3_conv_W):
    import numpy as np
    import concourse.bacc as bacc
    from concourse.bass_utils import run_bass_kernel_spmd

    nc = bacc.Bacc("TRN2", target_bir_lowering=False, num_devices=1, dynamic_dma_scratch_size=1024)
    dense, border = _layouts([np.asarray(w) for w in (L0_conv_W, L1_conv_W, L2_conv_W, L3_conv_W)])
    arrays = {"x_dram": np.ascontiguousarray(x), "dense_dram": dense, "border_dram": border, "const_dram": _constants()}
    args = [nc.dram_tensor(name, a.shape, mybir.dt.from_np(a.dtype), kind="ExternalInput").ap() for name, a in arrays.items()]
    out = nc.dram_tensor("out_dram", (B, C, H, W), F32, kind="ExternalOutput").ap()
    build(nc, *args, out)
    r = run_bass_kernel_spmd(nc, [arrays], core_ids=[0])
    return r.results[0]["out_dram"]
```

```python
from contextlib import ExitStack

import concourse.bass as bass
from concourse import mybir

F32 = mybir.dt.float32
F16 = mybir.dt.float16
BF16 = mybir.dt.bfloat16
U8 = mybir.dt.uint8
ALU = mybir.AluOpType
ACT = mybir.ActivationFunctionType
AX = mybir.AxisListType

P = 128
B, C, H, W = 16, 16, 384, 384
L = 4
KK = 3
BR = P // C
NB = H // BR
CB = 4
NC = NB // CB
CH = CB * W
RING = 4
WP = W + 2
HS = BR * C * KK
GROUP = 2
GN = GROUP * H * W
AN = (H // KK) * (W // KK)
NR = KK * KK
EPS = 1e-5
WSCALE = 64.0
SMALL = 384

NMASK = KK * BR
NATT = 2 * NR
CONSTS = 3 * P + NMASK + 2

MEAN_INCS = 2
PREP_INCS = 11
SCALE_INCS = 2
SPREAD_INCS = 5
WEIGHT_INCS = 5
MODULATIONS = 3
HALO_DMAS = [6, 4, 4, 6]
CHUNK_DMAS = CB


class Schedule:

    def __init__(self, mean_after, stats_after, counts, variances, splits):
        self.mean_after = mean_after
        self.stats_after = stats_after
        self.counts = counts
        self.variances = variances
        self.splits = splits


RESIDENT = Schedule(
    0, 8,
    {0: [0], 1: [1], 2: [2], 3: [3], 4: [4], 5: [5], 6: [6, 7], 7: [8]},
    {s: [2 * s - 2, 2 * s - 1] for s in range(1, 7)},
    {s: [s + RING] for s in range(NC)},
)
ARRIVING = Schedule(
    2, 9,
    {2: [0], 3: [1], 4: [2], 5: [3], 6: [4, 5], 7: [6, 7], 8: [8]},
    {3: [0, 1], 4: [2, 3], 5: [4, 5], 6: [6, 7], 7: [8, 9], 8: [10, 11]},
    {**{s: [s + RING] for s in range(NC - RING)}, 8: [], 9: [12, 13], 10: [14], 11: [15]},
)
SUM_LAG = 3


def build(nc, x_in, dense_in, border_in, const_in, out):
    with ExitStack() as ctx:
        def sb(name, shape, dt):
            return ctx.enter_context(nc.sbuf_tensor(name, shape, dt))

        def sem(name):
            return ctx.enter_context(nc.semaphore(name))

        img = [sb(f"image{p}", [P, NC * CH], F32) for p in range(2)]
        split = sb("split", [P, 2, RING * CB, WP], F16)
        halo = sb("halo", [96, RING * CB, WP], F16)
        normed = sb("normed", [P, CH], F32)
        wdense = [sb(f"wdense{p}", [P, 2, HS], F16) for p in range(2)]
        wborder = [sb(f"wborder{p}", [96, HS], F16) for p in range(2)]
        dense = sb("dense", [P, HS], F32)
        border = sb("border", [96, HS], F32)
        const = sb("const", [P, CONSTS], F32)
        zeros = sb("zeros", [32, WP], F16)
        over = sb("over", [P, CB * CB * (W // KK)], U8)
        dump = [sb(f"dump{i}", [P, CH], BF16) for i in range(3)]
        sums = [sb(f"sums{p}", [P, NC], F32) for p in range(2)]
        squares = sb("squares", [P, NC], F32)
        counts = sb("counts", [P, NR], F32)
        mean = sb("mean", [P, 1], F32)
        negmean = sb("negmean", [P, 1], F32)
        stats = sb("stats", [P, NC + NATT], F32)
        var = sb("var", [P, 1], F32)
        vareps = sb("vareps", [P, 1], F32)
        scale = [sb(f"scale{p}", [P, 1], F32) for p in range(2)]
        shift = [sb(f"shift{p}", [P, 1], F32) for p in range(2)]
        top = sb("top", [P, 2], F32)
        att = [sb(f"att{i}", [P, 2, NR], F32) for i in range(6)]
        esum = sb("esum", [P, 2], F32)
        erec = sb("erec", [P, 2], F32)
        spread = [sb(f"spread{i}", [P, KK, BR], F32) for i in range(3)]
        ps = ctx.enter_context(nc.psum_tensor("ps", [P, 2, CB, 512], F32))

        group_m = const[:, 0:P]
        channel_m = const[:, P:2 * P]
        halo_channel_m = const[:, 2 * P:3 * P]
        mask = const[:, 3 * P:3 * P + NMASK].rearrange("p (k r) -> p k r", k=KK)
        neghalf = const[:, 3 * P + NMASK:3 * P + NMASK + 1]
        one = const[:, 3 * P + NMASK + 1:3 * P + NMASK + 2]

        const_loaded = sem("const_loaded")
        zeroed = sem("zeroed")
        loaded = [sem(f"loaded{i}") for i in range(4)]
        stored = [sem(f"stored{i}") for i in range(4)]
        fresh_summed = sem("fresh_summed")
        conv_done = sem("conv_done")
        banks_free = sem("banks_free")
        normed_done = sem("normed_done")
        high_done = sem("high_done")
        low_done = sem("low_done")
        halo_done = [sem(f"halo_done{i}") for i in range(RING)]
        mean_psum = sem("mean_psum")
        mean_ready = sem("mean_ready")
        counted = sem("counted")
        squared = sem("squared")
        stats_psum = sem("stats_psum")
        prep = sem("prep")
        scale_ready = sem("scale_ready")
        exps = sem("exps")
        spreaded = sem("spreaded")
        dense_loaded = sem("dense_loaded")
        modulated = sem("modulated")
        weights_ready = sem("weights_ready")

        def chunk(p, c):
            return img[p][:, c * CH:(c + 1) * CH]

        def max_zero(value):
            return max(value, 0) if isinstance(value, int) else value

        def rows4(ap):
            return ap.rearrange("p (b w) -> p b w", w=W)

        def ring_rows(part, slot):
            return split[:, part, slot * CB:(slot + 1) * CB, 1:1 + W]

        block = ctx.enter_context(nc.Block())

        @block.sync
        def _(sp):
            def transfer(p, c, image, store):
                for t in range(CB):
                    row = (c * CB + t) * BR
                    tensor = out if store else x_in
                    dram = tensor[bass.ds(image, 1), :, row:row + BR, :].rearrange("i c r w -> (i c) r w")
                    sram = img[p][:, c * CH + t * W:c * CH + (t + 1) * W]
                    if store:
                        sp.dma_start(dram, sram).then_inc(stored[c % 4], 16)
                    else:
                        sp.dma_start(sram, dram).then_inc(loaded[c % 4], 16)

            def store(p, c, pair, number):
                sp.wait_ge(banks_free, number + 3)
                transfer(p, c, 2 * pair + p, True)

            def load(p, c, pair):
                sp.wait_ge(stored[c % 4], 16 * CHUNK_DMAS * (3 * (2 * pair - 2 + p) + c // 4 + 1))
                transfer(p, c, 2 * pair + p, False)

            def to_halo(slot, side, to, n, both, high):
                cells = slice(to, to + n)
                sp.dma_start(halo[32 * side:32 * side + 32, cells, :], both).then_inc(halo_done[slot], 16)
                sp.dma_start(halo[64 + side:64 + side + 2 * C - 1:2, cells, :], high).then_inc(halo_done[slot], 16)

            def send(slot, t, n, side):
                at = slot * CB + t
                to = (at + 1 if side == 0 else at - 1) % (RING * CB)
                row = BR - 1 if side == 0 else 0
                to_halo(slot, side, to, n, split[row::BR, :, at:at + n, :], split[row::BR, 0, at:at + n, :])

            def send_zeros(slot, side, to):
                to_halo(slot, side, to, 1, zeros[:, :].unsqueeze(1), zeros[0:C, :].unsqueeze(1))

            def send_up(c, number):
                sp.wait_ge(high_done, number + 1)
                sp.wait_ge(low_done, number + 1)
                slot = c % RING
                if c == 0:
                    send_zeros(slot, 0, 0)
                elif slot == 0:
                    send(slot, 0, 1, 1)
                if slot == 0:
                    send(slot, 1, CB - 1, 1)
                else:
                    send(slot, 0, CB, 1)

            def send_down(c):
                slot = c % RING
                if slot < RING - 1:
                    send(slot, 0, CB, 0)
                else:
                    send(slot, 0, CB - 1, 0)
                    if c == NC - 1:
                        send_zeros(slot, 1, RING * CB - 1)
                    else:
                        send(slot, CB - 1, 1, 0)

            def load_weights(layer, k):
                sp.wait_ge(weights_ready, WEIGHT_INCS * (k + 1))
                sp.dma_start(dense[:, :], dense_in[bass.ds(layer, 1), :, :].rearrange("l p n -> (l p) n")).then_inc(dense_loaded, 16)
                sp.dma_start(border[:, :], border_in[bass.ds(layer, 1), :, :].rearrange("l p n -> (l p) n")).then_inc(dense_loaded, 16)

            def phase(sch, p, k, layer_after, jobs, last=False):
                for i in range(NC):
                    if i == 2:
                        load_weights(layer_after, k)
                    for q in sch.splits[i]:
                        send_up(q % NC, 12 * k + q)
                        if not (last and q == NC + RING - 1):
                            sp.wait_ge(conv_done, 12 * k + q - RING + 2)
                            send_down(q % NC)
                    for job, jp, c, which in jobs.get(i, []):
                        if job == "store":
                            store(jp, c, which, 12 * k + c)
                        else:
                            load(jp, c, which)

            sp.dma_start(const[:, :], const_in).then_inc(const_loaded, 16)
            sp.dma_start(dense[:, :], dense_in[0]).then_inc(dense_loaded, 16)
            sp.dma_start(border[:, :], border_in[0]).then_inc(dense_loaded, 16)
            first = [(p, c) for p in range(2) for c in range(NC)]
            for n, (p, c) in enumerate(first[:16]):
                if n >= 4:
                    sp.wait_ge(fresh_summed, n - 3)
                transfer(p, c, p, False)
            sp.wait_ge(zeroed, 5)
            for q in range(RING):
                send_up(q, q)
                if q == RING - 1:
                    sp.wait_ge(conv_done, 1)
                send_down(q)
            for n, (p, c) in enumerate(first):
                if n >= 16:
                    sp.wait_ge(fresh_summed, n - 3)
                    transfer(p, c, p, False)

            def head(pair):
                phase(ARRIVING, 0, 8 * pair, 0, {})
                phase(RESIDENT, 1, 8 * pair + 1, 1, {})

            def middle(pair):
                with sp.Fori(1, L - 1) as layer:
                    phase(RESIDENT, 0, 8 * pair + 2 * layer, layer, {})
                    phase(RESIDENT, 1, 8 * pair + 2 * layer + 1, layer + 1, {})

            def tail(pair, more):
                even = {i: [("store", 0, i, pair)] + ([("load", 0, i - 1, pair + 1)] if more and i else []) for i in range(NC)}
                odd = {i: [("store", 1, i, pair)] + ([("load", 1, i - 1, pair + 1)] if more and i else []) for i in range(NC)}
                if more:
                    odd[0].append(("load", 0, NC - 1, pair + 1))
                phase(RESIDENT, 0, 8 * pair + 6, L - 1, even)
                phase(ARRIVING, 1, 8 * pair + 7, 0, odd, last=not more)
                if more:
                    load(1, NC - 1, pair + 1)

            with sp.Fori(0, B // 2 - 1) as pair:
                head(pair)
                middle(pair)
                tail(pair, True)
            head(B // 2 - 1)
            middle(B // 2 - 1)
            tail(B // 2 - 1, False)
            for i in range(4):
                sp.wait_ge(stored[i], 16 * CHUNK_DMAS * (NC // 4) * B)

        @block.scalar
        def _(act):
            def fresh(p, c, image):
                act.wait_ge(loaded[c % 4], 16 * CHUNK_DMAS * (3 * image + c // 4 + 1))
                act.wait_ge(fresh_summed, NC * image + c)
                nc.scalar.activation(dump[2][:, :], chunk(p, c), ACT.Identity,
                                     accum_out=sums[p][:, c:c + 1]).then_inc(fresh_summed, 1)

            def square(p, c, n):
                act.wait_ge(mean_ready, MEAN_INCS * (n + 1))
                act.wait_ge(squared, max_zero(NC * n + c - 1))
                nc.scalar.activation(dump[c % 2][:, :], chunk(p, c), ACT.Square, bias=negmean[:, :],
                                     accum_out=squares[:, c:c + 1]).then_inc(squared, 1)

            def normalise(p, c, number, free=None):
                if free is not None:
                    act.wait_ge(conv_done, free)
                act.wait_ge(low_done, number)
                nc.scalar.activation(normed[:, :], chunk(p, c), ACT.Identity, bias=shift[p][:, :],
                                     scale=scale[p][:, :]).then_inc(normed_done, 1)
                nc.scalar.activation(ring_rows(0, c % RING), rows4(chunk(p, c)), ACT.Identity, bias=shift[p][:, :],
                                     scale=scale[p][:, :]).then_inc(high_done, 1)

            def exp_shares(n):
                act.wait_ge(prep, PREP_INCS * n + 5)
                nc.scalar.activation(att[1][:, :, :], att[0][:, :, :], ACT.Exp).then_inc(exps, 1)

            def exp_sigmoid(n):
                act.wait_ge(prep, PREP_INCS * n + 8)
                nc.scalar.activation(att[3][:, :, :], att[2][:, :, :], ACT.Exp, bias=one, scale=-float(NR)).then_inc(exps, 1)

            def phase(sch, p, k, sums_due):
                n = k + 1
                for i in range(NC):
                    if i == sch.stats_after:
                        exp_shares(n)
                        act.wait_ge(scale_ready, SCALE_INCS * (n + 1))
                    for q in sch.splits[i]:
                        normalise(p if q < NC else 1 - p, q % NC, 12 * k + q, 12 * k + q - RING + 1)
                    if i == sch.stats_after:
                        exp_sigmoid(n)
                    for fp, c, image in sums_due.get(i, []):
                        fresh(fp, c, image)
                    for c in sch.variances.get(i, []):
                        square(1 - p, c, n)

            act.wait_ge(const_loaded, 16)
            for c in range(NC):
                fresh(0, c, 0)
            for c in range(NC):
                square(0, c, 0)
            exp_shares(0)
            act.wait_ge(scale_ready, SCALE_INCS)
            act.wait_ge(zeroed, 5)
            for q in range(RING):
                normalise(0, q, q)
            exp_sigmoid(0)
            for c in range(NC - SUM_LAG):
                fresh(1, c, 1)

            def head(pair):
                phase(ARRIVING, 0, 8 * pair, {0: [(1, NC - 3, 2 * pair + 1)], 1: [(1, NC - 2, 2 * pair + 1), (1, NC - 1, 2 * pair + 1)]})
                phase(RESIDENT, 1, 8 * pair + 1, {})

            def middle(pair):
                with act.Fori(1, L - 1) as layer:
                    phase(RESIDENT, 0, 8 * pair + 2 * layer, {})
                    phase(RESIDENT, 1, 8 * pair + 2 * layer + 1, {})

            def tail(pair, more):
                even, odd = {}, {}
                if more:
                    even = {i: [(0, i - SUM_LAG, 2 * pair + 2)] for i in range(SUM_LAG, NC)}
                    odd = {i: [(1, i - SUM_LAG, 2 * pair + 3)] for i in range(SUM_LAG, NC)}
                    odd[0] = [(0, NC - 3, 2 * pair + 2)]
                    odd[1] = [(0, NC - 2, 2 * pair + 2), (0, NC - 1, 2 * pair + 2)]
                phase(RESIDENT, 0, 8 * pair + 6, even)
                if not more:
                    act.sem_inc(fresh_summed, NC)
                phase(ARRIVING, 1, 8 * pair + 7, odd)

            with act.Fori(0, B // 2 - 1) as pair:
                head(pair)
                middle(pair)
                tail(pair, True)
            head(B // 2 - 1)
            middle(B // 2 - 1)
            tail(B // 2 - 1, False)

        @block.vector
        def _(dve):
            def each(pair_of_values):
                return pair_of_values[:, :].unsqueeze(2).to_broadcast([P, 2, NR])

            def evacuate(p, c, number):
                dve.wait_ge(conv_done, number + 1)
                nc.vector.scalar_tensor_tensor(
                    out=rows4(chunk(p, c)), in0=ps[:, c % 2, :, 0:W], scalar=1.0 / WSCALE, in1=rows4(chunk(p, c)),
                    op0=ALU.mult, op1=ALU.add, accum_out=sums[p][:, c:c + 1]).then_inc(banks_free, 1)

            def low(c, number):
                dve.wait_ge(normed_done, number + 1)
                dve.wait_ge(high_done, number + 1)
                nc.vector.tensor_tensor(ring_rows(1, c % RING), rows4(normed[:, :]), ring_rows(0, c % RING),
                                        ALU.subtract).then_inc(low_done, 1)

            def take_mean(n, half):
                dve.wait_ge(mean_psum, n + 1)
                nc.vector.tensor_reduce(mean[:, :], ps[:, half, CB - 1, SMALL:SMALL + NC], AX.X, ALU.add).then_inc(mean_ready, 1)
                dve.wait_ge(mean_ready, MEAN_INCS * n + 1)
                nc.vector.tensor_scalar(negmean[:, :], mean[:, :], -1.0, None, ALU.mult).then_inc(mean_ready, 1)

            def count(p, r, n):
                v, h = divmod(r, KK)
                nb, w = NB // KK, W // KK
                dve.wait_ge(counted, NR * n + r)
                region = img[p][:, v * nb * W:(v + 1) * nb * W].rearrange("p (b w) -> p b w", w=W)[:, :, h * w:(h + 1) * w]
                nc.vector.tensor_scalar(over[:, :].rearrange("p (b w) -> p b w", w=w), region, mean[:, :], None,
                                        ALU.is_ge, ALU.add, accum_out=counts[:, r:r + 1]).then_inc(counted, 1)

            def take_stats(n, half):
                dve.wait_ge(stats_psum, n + 1)
                nc.vector.tensor_copy(stats[:, :], ps[:, half, CB - 1, SMALL:SMALL + NC + NATT]).then_inc(prep, 1)
                dve.wait_ge(prep, PREP_INCS * n + 1)
                shares = stats[:, NC:NC + NATT].rearrange("p (h r) -> p h r", h=2)
                nc.vector.tensor_reduce(var[:, :], stats[:, 0:NC], AX.X, ALU.add).then_inc(prep, 1)
                nc.vector.tensor_reduce(top[:, :], shares, AX.X, ALU.max).then_inc(prep, 1)
                dve.wait_ge(prep, PREP_INCS * n + 3)
                nc.vector.tensor_scalar(vareps[:, :], var[:, :], EPS, None, ALU.add).then_inc(prep, 1)
                nc.vector.tensor_tensor(att[0][:, :, :], shares, each(top), ALU.subtract).then_inc(prep, 1)

            def attention(n):
                dve.wait_ge(exps, 2 * n + 1)
                nc.vector.tensor_reduce(esum[:, :], att[1][:, :, :], AX.X, ALU.add).then_inc(prep, 1)
                dve.wait_ge(prep, PREP_INCS * n + 6)
                nc.vector.reciprocal(erec[:, :], esum[:, :]).then_inc(prep, 1)
                dve.wait_ge(prep, PREP_INCS * n + 7)
                nc.vector.tensor_tensor(att[2][:, :, :], att[1][:, :, :], each(erec), ALU.mult).then_inc(prep, 1)
                dve.wait_ge(exps, 2 * n + 2)
                nc.vector.tensor_scalar(att[4][:, :, :], att[3][:, :, :], 1.0, None, ALU.add).then_inc(prep, 1)
                dve.wait_ge(prep, PREP_INCS * n + 9)
                nc.vector.reciprocal(att[1][:, :, :], att[4][:, :, :]).then_inc(prep, 1)
                dve.wait_ge(prep, PREP_INCS * n + 10)
                nc.vector.tensor_scalar(att[5][:, :, :], att[1][:, :, :], WSCALE, WSCALE, ALU.mult, ALU.add).then_inc(prep, 1)

            def phase(sch, p, k):
                n = k + 1
                for i in range(NC):
                    evacuate(p, i, 12 * k + i)
                    if i == sch.mean_after:
                        take_mean(n, (i + 1) % 2)
                        dve.wait_ge(mean_ready, MEAN_INCS * (n + 1))
                    if i == sch.stats_after:
                        take_stats(n, (i + 1) % 2)
                    for q in sch.splits[i]:
                        low(q % NC, 12 * k + q)
                    if i == sch.stats_after:
                        attention(n)
                    for r in sch.counts.get(i, []):
                        count(1 - p, r, n)

            nc.vector.memset(split[:, :, :, :], 0.0).then_inc(zeroed, 1)
            nc.vector.memset(halo[:, :, :], 0.0).then_inc(zeroed, 1)
            nc.vector.memset(zeros[:, :], 0.0).then_inc(zeroed, 1)
            for p in range(2):
                nc.vector.memset(wborder[p][:, :], 0.0).then_inc(zeroed, 1)
            dve.sem_inc(banks_free, 2)
            take_mean(0, 0)
            dve.wait_ge(mean_ready, MEAN_INCS)
            for r in range(NR):
                count(0, r, 0)
            take_stats(0, 0)
            for q in range(RING):
                low(q, q)
            attention(0)

            with dve.Fori(0, B // 2) as pair:
                phase(ARRIVING, 0, 8 * pair)
                phase(RESIDENT, 1, 8 * pair + 1)
                with dve.Fori(1, L - 1) as layer:
                    phase(RESIDENT, 0, 8 * pair + 2 * layer)
                    phase(RESIDENT, 1, 8 * pair + 2 * layer + 1)
                phase(RESIDENT, 0, 8 * pair + 6)
                phase(ARRIVING, 1, 8 * pair + 7)

        @block.gpsimd
        def _(pool):
            def spread_attention(n):
                shape = [P, KK, BR]
                value = att[5][:, 0, :].rearrange("p (k x) -> p k x", k=KK)
                base = SPREAD_INCS * n
                pool.wait_ge(prep, PREP_INCS * (n + 1))
                for ky in range(KK):
                    nc.gpsimd.tensor_tensor(spread[ky][:, :, :], mask[:, ky, :].unsqueeze(1).to_broadcast(shape),
                                            value[:, ky, :].unsqueeze(2).to_broadcast(shape), ALU.mult).then_inc(spreaded, 1)
                pool.wait_ge(spreaded, base + 3)
                nc.gpsimd.tensor_tensor(spread[0][:, :, :], spread[0][:, :, :], spread[1][:, :, :], ALU.add).then_inc(spreaded, 1)
                pool.wait_ge(spreaded, base + 4)
                nc.gpsimd.tensor_tensor(spread[0][:, :, :], spread[0][:, :, :], spread[2][:, :, :], ALU.add).then_inc(spreaded, 1)
                pool.wait_ge(spreaded, base + 5)

            def prepare(p, n):
                pool.wait_ge(prep, PREP_INCS * n + 4)
                nc.gpsimd.tensor_tensor(scale[p][:, :], vareps[:, :], neghalf, ALU.pow).then_inc(scale_ready, 1)
                pool.wait_ge(scale_ready, SCALE_INCS * n + 1)
                nc.gpsimd.tensor_tensor(shift[p][:, :], negmean[:, :], scale[p][:, :], ALU.mult).then_inc(scale_ready, 1)
                spread_attention(n)
                pool.wait_ge(dense_loaded, 32 * (n + 1))
                ws = WEIGHT_INCS * n

                def banded(ap):
                    return ap.rearrange("p (x o r) -> p x o r", x=KK, o=C)

                factor = spread[0][:, :, :].unsqueeze(2).to_broadcast([P, KK, C, BR])
                nc.gpsimd.tensor_tensor(banded(wdense[p][:, 0, :]), banded(dense[:, :]), factor, ALU.mult).then_inc(weights_ready, 1)
                nc.gpsimd.tensor_tensor(banded(dense[:, :]), banded(dense[:, :]), factor, ALU.mult).then_inc(modulated, 1)
                for row, ky in ((0, 0), (BR - 1, KK - 1)):
                    value = att[5][0:96, 1, ky * KK:ky * KK + KK].unsqueeze(2).to_broadcast([96, KK, C])
                    taps = banded(border[:, :])[:, :, :, row]
                    nc.gpsimd.tensor_tensor(banded(wborder[p][:, :])[:, :, :, row], taps, value, ALU.mult).then_inc(weights_ready, 1)
                    nc.gpsimd.tensor_tensor(taps, taps, value, ALU.mult).then_inc(modulated, 1)
                pool.wait_ge(weights_ready, ws + 3)
                pool.wait_ge(modulated, MODULATIONS * (n + 1))
                nc.gpsimd.tensor_tensor(wdense[p][:, 1, :], dense[:, :], wdense[p][:, 0, :], ALU.subtract).then_inc(weights_ready, 1)
                pool.wait_ge(weights_ready, ws + 4)
                nc.gpsimd.tensor_tensor(wborder[p][64:96, :], border[64:96, :], wborder[p][64:96, :], ALU.subtract).then_inc(weights_ready, 1)
                pool.wait_ge(weights_ready, ws + WEIGHT_INCS)

            pool.wait_ge(const_loaded, 16)
            pool.wait_ge(zeroed, 5)
            prepare(0, 0)
            with pool.Fori(0, B // 2 * L) as m:
                prepare(1, 2 * m + 1)
                prepare(0, 2 * m + 2)

        @block.tensor
        def _(pe):
            def sum_means(p, n, half):
                nc.tensor.matmul(ps[:, half, CB - 1, SMALL:SMALL + NC], group_m, sums[p][:, :],
                                 start=True, stop=True).then_inc(mean_psum, 1)

            def sum_stats(n, half):
                pe.wait_ge(squared, NC * (n + 1))
                pe.wait_ge(counted, NR * (n + 1))
                nc.tensor.matmul(ps[:, half, CB - 1, SMALL:SMALL + NC], group_m, squares[:, :], start=True, stop=True)
                first = SMALL + NC
                nc.tensor.matmul(ps[:, half, CB - 1, first:first + NR], channel_m, counts[:, :], start=True, stop=True)
                nc.tensor.matmul(ps[:, half, CB - 1, first + NR:first + NATT], halo_channel_m, counts[:, :],
                                 start=True, stop=True).then_inc(stats_psum, 1)

            def convolve(p, c, number, guard=None):
                slot, half = c % RING, c % 2
                if c == 0:
                    pe.wait_ge(halo_done[0], 16 * HALO_DMAS[0] * (number // RING + 1))
                if c < NC - 1:
                    below = (slot + 1) % RING
                    pe.wait_ge(halo_done[below], 16 * HALO_DMAS[below] * ((number + 1) // RING + 1))
                pe.wait_ge(banks_free, number + 1)
                for t in range(CB):
                    if t == CB - 1 and guard is not None:
                        pe.wait_ge(*guard)
                    at = slot * CB + t
                    for kx in range(KK):
                        for w, v in ((1, 0), (0, 1), (0, 0)):
                            nc.tensor.matmul(ps[:, half, t, 0:W], wdense[p][:, w, kx * P:(kx + 1) * P],
                                             split[:, v, at, kx:kx + W], start=(kx == 0 and w == 1), stop=False)
                    for kx in range(KK):
                        last = nc.tensor.matmul(ps[:, half, t, 0:W], wborder[p][:, kx * P:(kx + 1) * P],
                                                halo[:, at, kx:kx + W], start=False, stop=(kx == KK - 1))
                last.then_inc(conv_done, 1)

            def phase(sch, p, k, wait_sums):
                n, g = k + 1, 12 * k
                pe.wait_ge(weights_ready, WEIGHT_INCS * (k + 1))
                for c in range(NC):
                    guard = None
                    if c == sch.mean_after + 1:
                        guard = (mean_ready, MEAN_INCS * n + 1)
                    if c == sch.stats_after + 1:
                        guard = (prep, PREP_INCS * n + 1)
                    convolve(p, c, g + c, guard)
                    if c == sch.mean_after:
                        pe.wait_ge(*wait_sums)
                        pe.wait_ge(banks_free, g + c + 2)
                        sum_means(1 - p, n, (c + 1) % 2)
                    if c == sch.stats_after:
                        pe.wait_ge(banks_free, g + c + 2)
                        sum_stats(n, (c + 1) % 2)

            def resident(p, k):
                phase(RESIDENT, p, k, (banks_free, 12 * k + 2))

            pe.wait_ge(const_loaded, 16)
            pe.wait_ge(fresh_summed, NC)
            sum_means(0, 0, 0)
            pe.wait_ge(mean_ready, 1)
            sum_stats(0, 0)
            pe.wait_ge(prep, 1)
            with pe.Fori(0, B // 2) as pair:
                phase(ARRIVING, 0, 8 * pair, (fresh_summed, NC * (2 * pair + 2)))
                resident(1, 8 * pair + 1)
                with pe.Fori(1, L - 1) as layer:
                    resident(0, 8 * pair + 2 * layer)
                    resident(1, 8 * pair + 2 * layer + 1)
                resident(0, 8 * pair + 6)
                phase(ARRIVING, 1, 8 * pair + 7, (fresh_summed, NC * (2 * pair + 3)))


def _layouts(weights):
    import numpy as np
    dense = np.zeros((L, C, BR, KK, C, BR), np.float32)
    border = np.zeros((L, 96, KK, C, BR), np.float32)
    for layer, w in enumerate(weights):
        for row_in in range(BR):
            for row_out in range(BR):
                ky = row_in - row_out + 1
                if 0 <= ky < KK:
                    dense[layer, :, row_in, :, :, row_out] = w[:, :, ky, :].transpose(1, 2, 0)
        for side in range(2):
            taps = w[:, :, (KK - 1) * side, :].transpose(1, 2, 0)
            for part in range(2):
                border[layer, 32 * side + part:32 * side + 32:2, :, :, (BR - 1) * side] = taps
            border[layer, 64 + side:96:2, :, :, (BR - 1) * side] = taps
    return dense.reshape(L, P, HS), border.reshape(L, 96, HS)


def _constants():
    import numpy as np
    part = np.arange(P)
    channel = part // BR
    halo_channel = part % 32 // 2
    const = np.zeros((P, CONSTS), np.float32)
    const[:, 0:P] = (channel[:, None] // GROUP == channel[None, :] // GROUP) / GN
    const[:, P:2 * P] = (channel[:, None] == channel[None, :]) / AN
    const[:, 2 * P:3 * P] = (channel[:, None] == halo_channel[None, :]) / AN
    mask = np.zeros((P, KK, BR), np.float32)
    for row_in in range(BR):
        for row_out in range(BR):
            if 0 <= row_in - row_out + 1 < KK:
                mask[row_in::BR, row_in - row_out + 1, row_out] = 1
    const[:, 3 * P:3 * P + NMASK] = mask.reshape(P, NMASK)
    const[:, 3 * P + NMASK] = -0.5
    const[:, 3 * P + NMASK + 1] = 1
    return const


def kernel(x, L0_conv_W, L1_conv_W, L2_conv_W, L3_conv_W):
    import numpy as np
    import concourse.bacc as bacc
    from concourse.bass_utils import run_bass_kernel_spmd

    nc = bacc.Bacc("TRN2", target_bir_lowering=False, num_devices=1, dynamic_dma_scratch_size=1024)
    dense, border = _layouts([np.asarray(w) for w in (L0_conv_W, L1_conv_W, L2_conv_W, L3_conv_W)])
    arrays = {"x_dram": np.ascontiguousarray(x), "dense_dram": dense, "border_dram": border, "const_dram": _constants()}
    args = [nc.dram_tensor(name, a.shape, mybir.dt.from_np(a.dtype), kind="ExternalInput").ap() for name, a in arrays.items()]
    out = nc.dram_tensor("out_dram", (B, C, H, W), F32, kind="ExternalOutput").ap()
    build(nc, *args, out)
    r = run_bass_kernel_spmd(nc, [arrays], core_ids=[0])
    return r.results[0]["out_dram"]
```

```python
from contextlib import ExitStack

import concourse.bass as bass
from concourse import mybir

F32 = mybir.dt.float32
F16 = mybir.dt.float16
BF16 = mybir.dt.bfloat16
U8 = mybir.dt.uint8
ALU = mybir.AluOpType
ACT = mybir.ActivationFunctionType
AX = mybir.AxisListType

P = 128
B, C, H, W = 16, 16, 384, 384
L = 4
KK = 3
BR = P // C
NB = H // BR
CB = 3
NC = NB // CB
CH = CB * W
RING = 8
CELLS = RING * CB
ROWS = (0, 7, 1, 2, 3, 4, 5, 6)
GROUPS = ((0, 4), (4, 9), (9, 13), (13, 16))
WP = W + 2
HS = BR * C * KK
GROUP = 2
GN = GROUP * H * W
AN = (H // KK) * (W // KK)
NR = KK * KK
EPS = 1e-5
WSCALE = 64.0
SMALL = 384

NMASK = KK * BR
CONSTS = 2 * P + NMASK + 2

MEAN_INCS = 2
PREP_INCS = 10
SCALE_INCS = 2
SPREAD_INCS = 5
WEIGHT_INCS = 4
MODULATIONS = 2
QUAD = RING // 2
PAIR = 2
FIRST_DMAS, SECOND_DMAS, QUAD_DMAS = 6, 4, 6
HALF_DMAS = (SECOND_DMAS + QUAD_DMAS, 2 * QUAD_DMAS)
GROUP_DMAS = BR


class Schedule:

    def __init__(self, mean_after, stats_after, counts, variances, splits, sends):
        self.mean_after = mean_after
        self.stats_after = stats_after
        self.counts = counts
        self.variances = variances
        self.splits = splits
        self.sends = sends


EARLY = {0: [6, 7], 1: [8, 9], **{i: [i + RING] for i in range(2, NC - RING)}}
RESIDENT = Schedule(
    0, 10,
    {i: [i] for i in range(NR)},
    {2: [0, 1], 3: [2, 3], 4: [4, 5], 5: [6, 7], 6: [8, 9], 7: [10], 8: [11, 12, 13], 9: [14, 15]},
    {**EARLY, 11: [16, 17], 12: [18, 19], 13: [20], 14: [21]},
    {0: [(4, QUAD)], 3: [(8, QUAD)], 7: [(12, QUAD)], 12: [(16, PAIR)], 13: [(18, PAIR)]},
)
ARRIVING = Schedule(
    4, 12,
    {4: [0], 5: [1], 6: [2], 7: [3], 8: [4], 9: [5], 10: [6], 11: [7, 8]},
    {5: [0, 1], 6: [2, 3], 7: [4, 5], 8: [6, 7, 8], 9: [9, 10, 11], 10: [12, 13], 11: [14, 15]},
    {**EARLY, 13: [16, 17], 14: [18, 19], 15: [20, 21]},
    {0: [(4, QUAD)], 3: [(8, QUAD)], 7: [(12, QUAD)], 14: [(16, PAIR), (18, PAIR)]},
)
SPLIT_AHEAD = 6
STORES = {4: [0], 9: [1], 13: [2], 16: [3]}
LOADS = {6: [0], 11: [1], 15: [2], 17: [3]}
LAST_SUMS = {16: [9, 10], 17: [11, 12], 19: [13, 14, 15]}
SUMS = ({9: [0, 1, 2, 3], 15: [4, 5, 6, 7, 8], **LAST_SUMS},
        {9: [0, 1, 2, 3], 11: [4, 5, 6], 15: [7, 8], **LAST_SUMS})


def build(nc, x_in, dense_in, border_in, const_in, out):
    with ExitStack() as ctx:
        def sb(name, shape, dt):
            return ctx.enter_context(nc.sbuf_tensor(name, shape, dt))

        def sem(name):
            return ctx.enter_context(nc.semaphore(name))

        img = [sb(f"image{p}", [P, NC * CH], F32) for p in range(2)]
        split = sb("split", [P, 2, CELLS, WP], F16)
        halo = sb("halo", [96, CELLS, WP], F16)
        normed = [sb(f"normed{i}", [P, CH], F32) for i in range(2)]
        wdense = [sb(f"wdense{p}", [P, 2, HS], F16) for p in range(2)]
        wborder = [sb(f"wborder{p}", [96, KK * 2 * C], F16) for p in range(2)]
        dense = sb("dense", [P, HS], F32)
        border = sb("border", [96, KK * 2 * C], F32)
        const = sb("const", [P, CONSTS], F32)
        zeros = sb("zeros", [32, WP], F16)
        over = sb("over", [P, NB // KK * (W // KK)], U8)
        dump = [sb(f"dump{i}", [P, CH], BF16) for i in range(2)]
        sums = [sb(f"sums{p}", [P, NC], F32) for p in range(2)]
        squares = sb("squares", [P, NC], F32)
        counts = sb("counts", [P, NR], F32)
        mean = sb("mean", [P, 1], F32)
        negmean = sb("negmean", [P, 1], F32)
        stats = sb("stats", [P, NC + NR], F32)
        var = sb("var", [P, 1], F32)
        vareps = sb("vareps", [P, 1], F32)
        scale = [sb(f"scale{p}", [P, 1], F32) for p in range(2)]
        shift = [sb(f"shift{p}", [P, 1], F32) for p in range(2)]
        top = sb("top", [P, 1], F32)
        att = [sb(f"att{i}", [P, NR], F32) for i in range(6)]
        esum = sb("esum", [P, 1], F32)
        erec = sb("erec", [P, 1], F32)
        spread = [sb(f"spread{i}", [P, KK, BR], F32) for i in range(3)]
        ps = ctx.enter_context(nc.psum_tensor("ps", [P, 2, CB + 1, 512], F32))

        group_m = const[:, 0:P]
        channel_m = const[:, P:2 * P]
        mask = const[:, 2 * P:2 * P + NMASK].rearrange("p (k r) -> p k r", k=KK)
        neghalf = const[:, 2 * P + NMASK:2 * P + NMASK + 1]
        one = const[:, 2 * P + NMASK + 1:2 * P + NMASK + 2]

        const_loaded = sem("const_loaded")
        zeroed = sem("zeroed")
        loaded = [[sem(f"loaded{p}_{g}") for g in range(len(GROUPS))] for p in range(2)]
        stored = [[sem(f"stored{p}_{g}") for g in range(len(GROUPS))] for p in range(2)]
        fresh_summed = sem("fresh_summed")
        conv_done = sem("conv_done")
        banks_free = sem("banks_free")
        normed_done = sem("normed_done")
        high_done = sem("high_done")
        low_done = sem("low_done")
        halo_done = [sem(f"halo_done{i}") for i in range(RING // QUAD)]
        halo_first = sem("halo_first")
        border_added = sem("border_added")
        mean_psum = sem("mean_psum")
        mean_ready = sem("mean_ready")
        counted = sem("counted")
        squared = sem("squared")
        stats_psum = sem("stats_psum")
        prep = sem("prep")
        scale_ready = sem("scale_ready")
        exps = sem("exps")
        spreaded = sem("spreaded")
        dense_loaded = sem("dense_loaded")
        modulated = sem("modulated")
        weights_ready = sem("weights_ready")

        def chunk(p, c):
            return img[p][:, c * CH:(c + 1) * CH]

        def by_row(ap):
            return ap.rearrange("p (b w) -> p b w", w=W)

        def ring_rows(part, slot):
            return split[:, part, slot * CB:(slot + 1) * CB, 1:1 + W]

        block = ctx.enter_context(nc.Block())

        @block.sync
        def _(sp):
            def transfer(p, g, image, store):
                first, end = GROUPS[g]
                tensor = out if store else x_in
                for slot in reversed(range(BR)):
                    row = first * CB * BR + ROWS[slot]
                    last = row + ((end - first) * CB - 1) * BR
                    dram = tensor[bass.ds(image, 1), :, row:last + 1:BR, :].rearrange("i c b w -> (i c) b w")
                    lane = 32 * (slot // 2) + slot % 2
                    sram = img[p][lane:lane + 2 * C - 1:2, first * CH:end * CH].rearrange("c (b w) -> c b w", w=W)
                    if store:
                        sp.dma_start(dram, sram).then_inc(stored[p][g], 16)
                    else:
                        sp.dma_start(sram, dram).then_inc(loaded[p][g], 16)

            def store(p, g, pair, k):
                sp.wait_ge(banks_free, NC * k + GROUPS[g][1] + 2)
                transfer(p, g, 2 * pair + p, True)

            def load(p, g, pair):
                sp.wait_ge(stored[p][g], 16 * GROUP_DMAS * pair)
                transfer(p, g, 2 * pair + p, False)

            def to_halo(done, side, to, n, both, high):
                cells = slice(to, to + n)
                sp.dma_start(halo[32 * side:32 * side + 32, cells, :], both).then_inc(done, 16)
                sp.dma_start(halo[64 + side:64 + side + 2 * C - 1:2, cells, :], high).then_inc(done, 16)

            def send(done, slot, t, n, side):
                at = slot * CB + t
                to = (at + 1 if side == 0 else at - 1) % CELLS
                lanes = slice(1 - side, 2 * C - side, 2)
                to_halo(done, side, to, n, split[lanes, :, at:at + n, :], split[lanes, 0, at:at + n, :])

            def send_zeros(done, side, to):
                to_halo(done, side, to, 1, zeros[:, :].unsqueeze(1), zeros[0:C, :].unsqueeze(1))

            def send_borders(c, n, number, slot_used):
                slot = c % RING
                done = halo_first if c == 0 else halo_done[slot // QUAD]
                sp.wait_ge(high_done, number + n)
                sp.wait_ge(low_done, number + n)
                if slot == 0:
                    if c == 0:
                        send_zeros(done, 0, 0)
                    else:
                        send(done, slot, 0, 1, 1)
                    send(done, slot, 1, n * CB - 1, 1)
                else:
                    send(done, slot, 0, n * CB, 1)
                if slot_used is not None:
                    sp.wait_ge(conv_done, slot_used)
                if slot + n < RING:
                    send(done, slot, 0, n * CB, 0)
                else:
                    send(done, slot, 0, n * CB - 1, 0)
                    if c + n == NC:
                        send_zeros(done, 1, CELLS - 1)
                    else:
                        send(done, slot, n * CB - 1, 1, 0)

            def load_weights(layer, k):
                sp.wait_ge(weights_ready, WEIGHT_INCS * (k + 1))
                sp.dma_start(dense[:, :], dense_in[bass.ds(layer, 1), :, :].rearrange("l p n -> (l p) n")).then_inc(dense_loaded, 16)
                sp.dma_start(border[:, :], border_in[bass.ds(layer, 1), :, :].rearrange("l p n -> (l p) n")).then_inc(dense_loaded, 16)

            def phase(sch, k, layer_after, jobs):
                for i in range(NC):
                    if i == 3:
                        load_weights(layer_after, k)
                    for job, p, g, pair, ago in jobs.get(i, []):
                        if job == "store":
                            store(p, g, pair, k - ago)
                    for q, n in sch.sends.get(i, []):
                        send_borders(q % NC, n, NC * k + q, NC * k + q + n - RING + 1)
                    for job, p, g, pair, ago in jobs.get(i, []):
                        if job == "load":
                            load(p, g, pair)

            sp.dma_start(const[:, :], const_in).then_inc(const_loaded, 16)
            sp.dma_start(dense[:, :], dense_in[0]).then_inc(dense_loaded, 16)
            sp.dma_start(border[:, :], border_in[0]).then_inc(dense_loaded, 16)
            for g in range(len(GROUPS)):
                transfer(0, g, 0, False)
            for g in range(len(GROUPS)):
                transfer(1, g, 1, False)
            sp.wait_ge(zeroed, 3)
            send_borders(0, PAIR, 0, None)
            send_borders(PAIR, PAIR, PAIR, None)

            def jobs_of(p, pair, more, base):
                jobs = {}
                for i in range(base, base + NC):
                    jobs[i - base] = ([("load", p, g, pair + 1, base // NC) for g in LOADS.get(i, []) if more]
                                      + [("store", p, g, pair, base // NC) for g in STORES.get(i, [])])
                return jobs

            def both(a, b):
                return {i: a.get(i, []) + b.get(i, []) for i in range(NC)}

            def head(pair, previous):
                phase(ARRIVING, 8 * pair, 0, jobs_of(1, pair - 1, True, NC) if previous else {})
                phase(RESIDENT, 8 * pair + 1, 1, {})

            def middle(pair):
                with sp.Fori(1, L - 1) as layer:
                    phase(RESIDENT, 8 * pair + 2 * layer, layer, {})
                    phase(RESIDENT, 8 * pair + 2 * layer + 1, layer + 1, {})

            def tail(pair, more):
                phase(RESIDENT, 8 * pair + 6, L - 1, jobs_of(0, pair, more, 0))
                phase(ARRIVING, 8 * pair + 7, 0, both(jobs_of(0, pair, more, NC), jobs_of(1, pair, more, 0)))

            head(0, False)
            middle(0)
            with sp.Fori(1, B // 2) as pair:
                tail(pair - 1, True)
                head(pair, True)
                middle(pair)
            tail(B // 2 - 1, False)
            for g in STORES[NC]:
                store(1, g, B // 2 - 1, L * B - 1)
            for p in range(2):
                for g in range(len(GROUPS)):
                    sp.wait_ge(stored[p][g], 16 * GROUP_DMAS * (B // 2))

        @block.scalar
        def _(act):
            def fresh(p, c, pair):
                g = [first <= c < end for first, end in GROUPS].index(True)
                act.wait_ge(loaded[p][g], 16 * GROUP_DMAS * (pair + 1))
                before = NC * (2 * pair + p) + c
                if not isinstance(before, int) or before:
                    act.wait_ge(fresh_summed, before)
                nc.scalar.activation(dump[1][:, :], chunk(p, c), ACT.Identity,
                                     accum_out=sums[p][:, c:c + 1]).then_inc(fresh_summed, 1)

            def square(p, c, n):
                act.wait_ge(mean_ready, MEAN_INCS * (n + 1))
                before = NC * n + c
                if not isinstance(before, int) or before:
                    act.wait_ge(squared, before)
                nc.scalar.activation(dump[0][:, :], chunk(p, c), ACT.Square, bias=negmean[:, :],
                                     accum_out=squares[:, c:c + 1]).then_inc(squared, 1)

            def slot_free(k, q):
                if q < RING:
                    return banks_free, NC * k + q - RING + 3
                return conv_done, NC * k + q - RING + 1

            def normalise(p, c, number, free=None):
                if free is not None:
                    act.wait_ge(*free)
                if not isinstance(number, int) or number >= 2:
                    act.wait_ge(low_done, number - 1)
                nc.scalar.activation(normed[c % 2][:, :], chunk(p, c), ACT.Identity, bias=shift[p][:, :],
                                     scale=scale[p][:, :]).then_inc(normed_done, 1)
                nc.scalar.activation(ring_rows(0, c % RING), by_row(chunk(p, c)), ACT.Identity, bias=shift[p][:, :],
                                     scale=scale[p][:, :]).then_inc(high_done, 1)

            def exp_shares(n):
                act.wait_ge(prep, PREP_INCS * n + 5)
                nc.scalar.activation(att[1][:, :], att[0][:, :], ACT.Exp, accum_out=esum[:, :]).then_inc(exps, 1)

            def exp_sigmoid(n):
                act.wait_ge(prep, PREP_INCS * n + 7)
                nc.scalar.activation(att[3][:, :], att[2][:, :], ACT.Exp, bias=one, scale=-float(NR)).then_inc(exps, 1)

            def phase(sch, p, k, sums_due):
                n = k + 1
                for i in range(NC):
                    if i == sch.stats_after:
                        exp_shares(n)
                        exp_sigmoid(n)
                        act.wait_ge(scale_ready, SCALE_INCS * (n + 1))
                    for q in sch.splits.get(i, []):
                        normalise(p if q < NC else 1 - p, q % NC, NC * k + q, slot_free(k, q))
                    for c in sch.variances.get(i, []):
                        square(1 - p, c, n)
                    for fp, c, pair in sums_due.get(i, []):
                        fresh(fp, c, pair)

            act.wait_ge(const_loaded, 16)
            for c in range(NC):
                fresh(0, c, 0)
            for c in range(NC):
                square(0, c, 0)
            exp_shares(0)
            exp_sigmoid(0)
            act.wait_ge(scale_ready, SCALE_INCS)
            act.wait_ge(zeroed, 3)
            for q in range(SPLIT_AHEAD):
                normalise(0, q, q)

            def sums_of(p, pair, base):
                return {i - base: [(p, c, pair + 1) for c in SUMS[p].get(i, [])] for i in range(base, base + NC)}

            def both(a, b):
                return {i: a.get(i, []) + b.get(i, []) for i in range(NC)}

            def head(pair, due):
                phase(ARRIVING, 0, 8 * pair, due)
                phase(RESIDENT, 1, 8 * pair + 1, {})

            def middle(pair):
                with act.Fori(1, L - 1) as layer:
                    phase(RESIDENT, 0, 8 * pair + 2 * layer, {})
                    phase(RESIDENT, 1, 8 * pair + 2 * layer + 1, {})

            head(0, {i: [(1, c, 0) for c in range(4 * i, 4 * i + 4)] for i in range(4)})
            middle(0)
            with act.Fori(1, B // 2) as pair:
                phase(RESIDENT, 0, 8 * pair - 2, sums_of(0, pair - 1, 0))
                phase(ARRIVING, 1, 8 * pair - 1, both(sums_of(0, pair - 1, NC), sums_of(1, pair - 1, 0)))
                head(pair, sums_of(1, pair - 1, NC))
                middle(pair)
            phase(RESIDENT, 0, 4 * B - 2, {})
            act.sem_inc(fresh_summed, NC)
            phase(ARRIVING, 1, 4 * B - 1, {})

        @block.vector
        def _(dve):
            def evacuate(p, c, number):
                dve.wait_ge(conv_done, number + 1)
                for t in range(CB):
                    rows = img[p][0:32, c * CH + t * W:c * CH + (t + 1) * W]
                    nc.vector.scalar_tensor_tensor(
                        out=rows, in0=ps[32 * t:32 * t + 32, c % 2, CB, 0:W], scalar=1.0 / WSCALE, in1=rows,
                        op0=ALU.mult, op1=ALU.add).then_inc(border_added, 1)
                dve.wait_ge(border_added, CB * (number + 1))
                nc.vector.scalar_tensor_tensor(
                    out=by_row(chunk(p, c)), in0=ps[:, c % 2, 0:CB, 0:W], scalar=1.0 / WSCALE, in1=by_row(chunk(p, c)),
                    op0=ALU.mult, op1=ALU.add, accum_out=sums[p][:, c:c + 1]).then_inc(banks_free, 1)

            def take_mean(n, half):
                dve.wait_ge(mean_psum, n + 1)
                nc.vector.tensor_reduce(mean[:, :], ps[:, half, CB, SMALL:SMALL + NC], AX.X, ALU.add).then_inc(mean_ready, 1)
                dve.wait_ge(mean_ready, MEAN_INCS * n + 1)
                nc.vector.tensor_scalar(negmean[:, :], mean[:, :], -1.0, None, ALU.mult).then_inc(mean_ready, 1)

            def count(p, r, n):
                v, h = divmod(r, KK)
                nb, w = NB // KK, W // KK
                dve.wait_ge(counted, NR * n + r)
                region = img[p][:, v * nb * W:(v + 1) * nb * W].rearrange("p (b w) -> p b w", w=W)[:, :, h * w:(h + 1) * w]
                nc.vector.tensor_scalar(over[:, :].rearrange("p (b w) -> p b w", w=w), region, mean[:, :], None,
                                        ALU.is_ge, ALU.add, accum_out=counts[:, r:r + 1]).then_inc(counted, 1)

            def take_stats(n, half):
                dve.wait_ge(stats_psum, n + 1)
                nc.vector.tensor_copy(stats[:, :], ps[:, half, CB, SMALL:SMALL + NC + NR]).then_inc(prep, 1)
                dve.wait_ge(prep, PREP_INCS * n + 1)
                nc.vector.tensor_reduce(var[:, :], stats[:, 0:NC], AX.X, ALU.add).then_inc(prep, 1)
                nc.vector.tensor_reduce(top[:, :], stats[:, NC:NC + NR], AX.X, ALU.max).then_inc(prep, 1)
                dve.wait_ge(prep, PREP_INCS * n + 3)
                nc.vector.tensor_scalar(vareps[:, :], var[:, :], EPS, None, ALU.add).then_inc(prep, 1)
                nc.vector.tensor_scalar(att[0][:, :], stats[:, NC:NC + NR], top[:, :], None, ALU.subtract).then_inc(prep, 1)

            def attention(n):
                dve.wait_ge(exps, 2 * n + 1)
                nc.vector.reciprocal(erec[:, :], esum[:, :]).then_inc(prep, 1)
                dve.wait_ge(prep, PREP_INCS * n + 6)
                nc.vector.tensor_scalar(att[2][:, :], att[1][:, :], erec[:, :], None, ALU.mult).then_inc(prep, 1)
                dve.wait_ge(exps, 2 * n + 2)
                nc.vector.tensor_scalar(att[4][:, :], att[3][:, :], 1.0, None, ALU.add).then_inc(prep, 1)
                dve.wait_ge(prep, PREP_INCS * n + 8)
                nc.vector.reciprocal(att[1][:, :], att[4][:, :]).then_inc(prep, 1)
                dve.wait_ge(prep, PREP_INCS * n + 9)
                nc.vector.tensor_scalar(att[5][:, :], att[1][:, :], WSCALE, WSCALE, ALU.mult, ALU.add).then_inc(prep, 1)

            def low(c, number):
                dve.wait_ge(normed_done, number + 1)
                dve.wait_ge(high_done, number + 1)
                if c == 0 and not isinstance(number, int):
                    dve.wait_ge(low_done, number)
                nc.vector.tensor_tensor(ring_rows(1, c % RING), by_row(normed[c % 2][:, :]), ring_rows(0, c % RING),
                                        ALU.subtract).then_inc(low_done, 1)

            def phase(sch, p, k):
                n = k + 1
                for i in range(NC):
                    evacuate(p, i, NC * k + i)
                    if i == sch.mean_after:
                        take_mean(n, (i + 1) % 2)
                        dve.wait_ge(mean_ready, MEAN_INCS * (n + 1))
                    if i == sch.stats_after:
                        take_stats(n, (i + 1) % 2)
                        attention(n)
                    for r in sch.counts.get(i, []):
                        count(1 - p, r, n)
                    for q in sch.splits.get(i, []):
                        if q >= NC:
                            low(q - NC, NC * k + q)

            nc.vector.memset(split[:, :, :, :], 0.0).then_inc(zeroed, 1)
            nc.vector.memset(halo[:, :, :], 0.0).then_inc(zeroed, 1)
            nc.vector.memset(zeros[:, :], 0.0).then_inc(zeroed, 1)
            dve.sem_inc(banks_free, 2)
            take_mean(0, 0)
            dve.wait_ge(mean_ready, MEAN_INCS)
            for r in range(NR):
                count(0, r, 0)
            take_stats(0, 0)
            attention(0)
            for q in range(SPLIT_AHEAD):
                low(q, q)

            with dve.Fori(0, B // 2) as pair:
                phase(ARRIVING, 0, 8 * pair)
                phase(RESIDENT, 1, 8 * pair + 1)
                with dve.Fori(1, L - 1) as layer:
                    phase(RESIDENT, 0, 8 * pair + 2 * layer)
                    phase(RESIDENT, 1, 8 * pair + 2 * layer + 1)
                phase(RESIDENT, 0, 8 * pair + 6)
                phase(ARRIVING, 1, 8 * pair + 7)

        @block.gpsimd
        def _(pool):
            def spread_attention(n):
                shape = [P, KK, BR]
                value = att[5][:, :].rearrange("p (k x) -> p k x", k=KK)
                base = SPREAD_INCS * n
                pool.wait_ge(prep, PREP_INCS * (n + 1))
                for ky in range(KK):
                    nc.gpsimd.tensor_tensor(spread[ky][:, :, :], mask[:, ky, :].unsqueeze(1).to_broadcast(shape),
                                            value[:, ky, :].unsqueeze(2).to_broadcast(shape), ALU.mult).then_inc(spreaded, 1)
                pool.wait_ge(spreaded, base + 3)
                nc.gpsimd.tensor_tensor(spread[0][:, :, :], spread[0][:, :, :], spread[1][:, :, :], ALU.add).then_inc(spreaded, 1)
                pool.wait_ge(spreaded, base + 4)
                nc.gpsimd.tensor_tensor(spread[0][:, :, :], spread[0][:, :, :], spread[2][:, :, :], ALU.add).then_inc(spreaded, 1)
                pool.wait_ge(spreaded, base + 5)

            def make_scale(p, n):
                pool.wait_ge(prep, PREP_INCS * n + 4)
                nc.gpsimd.tensor_tensor(scale[p][:, :], vareps[:, :], neghalf, ALU.pow).then_inc(scale_ready, 1)
                pool.wait_ge(scale_ready, SCALE_INCS * n + 1)
                nc.gpsimd.tensor_tensor(shift[p][:, :], negmean[:, :], scale[p][:, :], ALU.mult).then_inc(scale_ready, 1)

            def make_weights(p, n):
                spread_attention(n)
                pool.wait_ge(dense_loaded, 32 * (n + 1))
                ws = WEIGHT_INCS * n

                def by_slot(ap):
                    return ap.rearrange("p (a o s) -> p a o s", o=C, s=2)

                factor = spread[0][:, :, :].rearrange("p x (q s) -> p (x q) s", s=2).unsqueeze(2)
                factor = factor.to_broadcast([P, KK * BR // 2, C, 2])
                nc.gpsimd.tensor_tensor(by_slot(wdense[p][:, 0, :]), by_slot(dense[:, :]), factor, ALU.mult).then_inc(weights_ready, 1)
                nc.gpsimd.tensor_tensor(by_slot(dense[:, :]), by_slot(dense[:, :]), factor, ALU.mult).then_inc(modulated, 1)
                value = att[5][0:96, :].rearrange("p (k x) -> p x k", k=KK)[:, :, 0:KK:2].unsqueeze(2).to_broadcast([96, KK, C, 2])
                nc.gpsimd.tensor_tensor(by_slot(wborder[p][:, :]), by_slot(border[:, :]), value, ALU.mult).then_inc(weights_ready, 1)
                nc.gpsimd.tensor_tensor(by_slot(border[:, :]), by_slot(border[:, :]), value, ALU.mult).then_inc(modulated, 1)
                pool.wait_ge(weights_ready, ws + 2)
                pool.wait_ge(modulated, MODULATIONS * (n + 1))
                nc.gpsimd.tensor_tensor(wdense[p][:, 1, :], dense[:, :], wdense[p][:, 0, :], ALU.subtract).then_inc(weights_ready, 1)
                pool.wait_ge(weights_ready, ws + 3)
                nc.gpsimd.tensor_tensor(wborder[p][64:96, :], border[64:96, :], wborder[p][64:96, :], ALU.subtract).then_inc(weights_ready, 1)

            def low(c, number, k):
                pool.wait_ge(normed_done, number + 1)
                pool.wait_ge(high_done, number + 1)
                if c == SPLIT_AHEAD:
                    pool.wait_ge(low_done, number)
                    pool.wait_ge(weights_ready, WEIGHT_INCS * (k + 1))
                nc.gpsimd.tensor_tensor(ring_rows(1, c % RING), by_row(normed[c % 2][:, :]), ring_rows(0, c % RING),
                                        ALU.subtract).then_inc(low_done, 1)

            def phase(sch, p, k):
                for i in range(NC):
                    if i == sch.stats_after:
                        make_scale(1 - p, k + 1)
                        make_weights(1 - p, k + 1)
                    for q in sch.splits.get(i, []):
                        if q < NC:
                            low(q, NC * k + q, k)

            pool.wait_ge(const_loaded, 16)
            make_scale(0, 0)
            make_weights(0, 0)

            with pool.Fori(0, B // 2) as pair:
                phase(ARRIVING, 0, 8 * pair)
                phase(RESIDENT, 1, 8 * pair + 1)
                with pool.Fori(1, L - 1) as layer:
                    phase(RESIDENT, 0, 8 * pair + 2 * layer)
                    phase(RESIDENT, 1, 8 * pair + 2 * layer + 1)
                phase(RESIDENT, 0, 8 * pair + 6)
                phase(ARRIVING, 1, 8 * pair + 7)

        @block.tensor
        def _(pe):
            def sum_means(p, n, half):
                nc.tensor.matmul(ps[:, half, CB, SMALL:SMALL + NC], group_m, sums[p][:, :],
                                 start=True, stop=True).then_inc(mean_psum, 1)

            def sum_stats(n, half):
                pe.wait_ge(squared, NC * (n + 1))
                pe.wait_ge(counted, NR * (n + 1))
                nc.tensor.matmul(ps[:, half, CB, SMALL:SMALL + NC], group_m, squares[:, :], start=True, stop=True)
                nc.tensor.matmul(ps[:, half, CB, SMALL + NC:SMALL + NC + NR], channel_m, counts[:, :],
                                 start=True, stop=True).then_inc(stats_psum, 1)

            def convolve(p, c, k, guard=None):
                slot, half, number = c % RING, c % 2, NC * k + c
                if c == 0:
                    pe.wait_ge(halo_first, 16 * FIRST_DMAS * (k + 1))
                elif c == 1:
                    pe.wait_ge(halo_done[0], 16 * HALF_DMAS[0] * k + 16 * SECOND_DMAS)
                elif c == QUAD - 1:
                    pe.wait_ge(halo_done[1], 16 * HALF_DMAS[1] * k + 16 * QUAD_DMAS)
                elif c == 2 * QUAD - 1:
                    pe.wait_ge(halo_done[0], 16 * HALF_DMAS[0] * (k + 1))
                elif c == 3 * QUAD - 1:
                    pe.wait_ge(halo_done[1], 16 * HALF_DMAS[1] * (k + 1))
                pe.wait_ge(banks_free, number + 1)
                for t in range(CB):
                    at = slot * CB + t
                    for kx in range(KK):
                        for w, v in ((1, 0), (0, 1), (0, 0)):
                            nc.tensor.matmul(ps[:, half, t, 0:W], wdense[p][:, w, kx * P:(kx + 1) * P],
                                             split[:, v, at, kx:kx + W], start=(kx == 0 and w == 1), stop=(kx == KK - 1 and v + w == 0))
                if guard is not None:
                    pe.wait_ge(*guard)
                for kx in range(KK):
                    for t in range(CB):
                        last = nc.tensor.matmul(ps[32 * t:32 * t + 32, half, CB, 0:W], wborder[p][:, kx * 2 * C:(kx + 1) * 2 * C],
                                                halo[:, slot * CB + t, kx:kx + W], start=(kx == 0), stop=(kx == KK - 1))
                last.then_inc(conv_done, 1)

            def phase(sch, p, k, wait_sums):
                n, g = k + 1, NC * k
                pe.wait_ge(weights_ready, WEIGHT_INCS * (k + 1))
                for c in range(NC):
                    guard = None
                    if c == sch.mean_after + 1:
                        guard = (mean_ready, MEAN_INCS * n + 1)
                    if c == sch.stats_after + 1:
                        guard = (prep, PREP_INCS * n + 1)
                    convolve(p, c, k, guard)
                    if c == sch.mean_after:
                        pe.wait_ge(*wait_sums)
                        pe.wait_ge(banks_free, g + c + 2)
                        sum_means(1 - p, n, (c + 1) % 2)
                    if c == sch.stats_after:
                        pe.wait_ge(banks_free, g + c + 2)
                        sum_stats(n, (c + 1) % 2)

            def resident(p, k):
                phase(RESIDENT, p, k, (banks_free, NC * k + 2))

            pe.wait_ge(const_loaded, 16)
            pe.wait_ge(fresh_summed, NC)
            sum_means(0, 0, 0)
            pe.wait_ge(mean_ready, 1)
            sum_stats(0, 0)
            pe.wait_ge(prep, 1)
            with pe.Fori(0, B // 2) as pair:
                phase(ARRIVING, 0, 8 * pair, (fresh_summed, NC * (2 * pair + 2)))
                resident(1, 8 * pair + 1)
                with pe.Fori(1, L - 1) as layer:
                    resident(0, 8 * pair + 2 * layer)
                    resident(1, 8 * pair + 2 * layer + 1)
                resident(0, 8 * pair + 6)
                phase(ARRIVING, 1, 8 * pair + 7, (fresh_summed, NC * (2 * pair + 3)))


def _layouts(weights):
    import numpy as np
    dense = np.zeros((L, BR // 2, C, 2, KK, BR // 2, C, 2), np.float32)
    border = np.zeros((L, 96, KK, C, 2), np.float32)
    for layer, w in enumerate(weights):
        for si, ri in enumerate(ROWS):
            for so, ro in enumerate(ROWS):
                if 0 <= ri - ro + 1 < KK:
                    dense[layer, si // 2, :, si % 2, :, so // 2, :, so % 2] = w[:, :, ri - ro + 1, :].transpose(1, 2, 0)
        for side in range(2):
            taps = w[:, :, (KK - 1) * side, :].transpose(1, 2, 0)
            for part in range(2):
                border[layer, 32 * side + part:32 * side + 32:2, :, :, side] = taps
            border[layer, 64 + side:96:2, :, :, side] = taps
    return dense.reshape(L, P, HS), border.reshape(L, 96, KK * 2 * C)


def _constants():
    import numpy as np
    channel = np.arange(P) % 32 // 2
    const = np.zeros((P, CONSTS), np.float32)
    const[:, 0:P] = (channel[:, None] // GROUP == channel[None, :] // GROUP) / GN
    const[:, P:2 * P] = (channel[:, None] == channel[None, :]) / AN
    mask = np.zeros((P, KK, BR), np.float32)
    for si, ri in enumerate(ROWS):
        for so, ro in enumerate(ROWS):
            if 0 <= ri - ro + 1 < KK:
                mask[32 * (si // 2) + si % 2:32 * (si // 2) + 32:2, ri - ro + 1, so] = 1
    const[:, 2 * P:2 * P + NMASK] = mask.reshape(P, NMASK)
    const[:, 2 * P + NMASK] = -0.5
    const[:, 2 * P + NMASK + 1] = 1
    return const


def kernel(x, L0_conv_W, L1_conv_W, L2_conv_W, L3_conv_W):
    import numpy as np
    import concourse.bacc as bacc
    from concourse.bass_utils import run_bass_kernel_spmd

    nc = bacc.Bacc("TRN2", target_bir_lowering=False, num_devices=1, dynamic_dma_scratch_size=1024)
    dense, border = _layouts([np.asarray(w) for w in (L0_conv_W, L1_conv_W, L2_conv_W, L3_conv_W)])
    arrays = {"x_dram": np.ascontiguousarray(x), "dense_dram": dense, "border_dram": border, "const_dram": _constants()}
    args = [nc.dram_tensor(name, a.shape, mybir.dt.from_np(a.dtype), kind="ExternalInput").ap() for name, a in arrays.items()]
    out = nc.dram_tensor("out_dram", (B, C, H, W), F32, kind="ExternalOutput").ap()
    build(nc, *args, out)
    r = run_bass_kernel_spmd(nc, [arrays], core_ids=[0])
    return r.results[0]["out_dram"]
```
